# Optimizing a Trainium2 kernel written in Bass

```python
import numpy as np
import jax
import jax.numpy as jnp

def _softmax(x, axis=-1):
    return jax.nn.softmax(x, axis=axis)

def _gelu(x):
    return jax.nn.gelu(x, approximate=True)

def _silu(x):
    return jax.nn.silu(x)

def _sigmoid(x):
    return jax.nn.sigmoid(x)

def _layernorm(x, axis=-1, eps=1e-05):
    m = jnp.mean(x, axis=axis, keepdims=True)
    v = jnp.var(x, axis=axis, keepdims=True)
    return (x - m) / jnp.sqrt(v + eps)

def _scatter_add(tgt, idx, src, axis=0):
    return tgt.at[idx].add(src)

def _segment_sum(src, seg, n):
    return jax.ops.segment_sum(src, seg, n)
kernel_name = 'mk_cond_resid_d1_seqx_r2_7e819d'

def setup_inputs(seed: int=0):
    np.random.seed(seed)
    _w = jnp.asarray

    def _rec_inputs():
        import jax
        import jax.numpy as jnp
        _rk = jax.random.key(seed)
        x = -0.000125 + 0.9999 * jax.random.normal(jax.random.fold_in(_rk, 1), (8, 512, 512), jnp.float32)
        _lenS = 512 - jax.random.randint(jax.random.fold_in(_rk, 7), (8,), 0, max(1, 512 // 4) + 1, jnp.int32)
        _lenS2 = 512 - jax.random.randint(jax.random.fold_in(_rk, 8), (8,), 0, max(1, 512 // 4) + 1, jnp.int32)
        cond_1024 = -0.00493535 + 1.00056 * jax.random.normal(jax.random.fold_in(_rk, 11), (8, 512), jnp.float32)
        return (x, cond_1024)
    x, cond_1024 = _rec_inputs()

    def _L0_cond_setup():
        import jax, jax.numpy as jnp
        import numpy as np
        import math
        N, T, D, H = (64, 256, 512, 512)

        def lstm_forward(x, h0, Wx, Wh, b):
            Hd = h0.shape[1]
            xW = jnp.einsum('ntd,dg->ntg', x, Wx) + b
            c0 = jnp.zeros_like(h0)

            def step(carry, xw_t):
                prev_h, prev_c = carry
                a = xw_t + prev_h @ Wh
                i = jax.nn.sigmoid(a[:, :Hd])
                f = jax.nn.sigmoid(a[:, Hd:2 * Hd])
                o = jax.nn.sigmoid(a[:, 2 * Hd:3 * Hd])
                g = jnp.tanh(a[:, 3 * Hd:])
                next_c = f * prev_c + i * g
                next_h = o * jnp.tanh(next_c)
                return ((next_h, next_c), next_h)
            (_, _), hs = jax.lax.scan(step, (h0, c0), jnp.swapaxes(xW, 0, 1))
            return jnp.swapaxes(hs, 0, 1)
        key = jax.random.key(seed)
        k1, k2, k3, k4 = jax.random.split(key, 4)
        x = jax.random.normal(k1, (N, T, D), dtype=jnp.float32)
        h0 = jax.random.normal(k2, (N, H), dtype=jnp.float32)
        Wx = jax.random.normal(k3, (D, 4 * H), dtype=jnp.float32) / math.sqrt(D)
        Wh = jax.random.normal(k4, (H, 4 * H), dtype=jnp.float32) / math.sqrt(H)
        b = jnp.zeros((4 * H,), dtype=jnp.float32)
        return {'x': x, 'h0': h0, 'Wx': Wx, 'Wh': Wh, 'b': b}
    _L0_cond_all = _L0_cond_setup()
    _L0_cond_in = {k: v for k, v in _L0_cond_all.items() if k in ('Wx', 'Wh', 'b')}
    del _L0_cond_all
    return {'x': x, 'cond_1024': cond_1024, 'L0_cond_Wx': _L0_cond_in['Wx'], 'L0_cond_Wh': _L0_cond_in['Wh'], 'L0_cond_b': _L0_cond_in['b']}

def reference(x, cond_1024, L0_cond_Wx, L0_cond_Wh, L0_cond_b):
    import jax
    import jax.numpy as jnp

    def _L0_cond_ref(x, h0, Wx, Wh, b):
        import jax, jax.numpy as jnp
        import numpy as np
        import math
        N, T, D, H = (64, 256, 512, 512)

        def lstm_forward(x, h0, Wx, Wh, b):
            Hd = h0.shape[1]
            xW = jnp.einsum('ntd,dg->ntg', x, Wx) + b
            c0 = jnp.zeros_like(h0)

            def step(carry, xw_t):
                prev_h, prev_c = carry
                a = xw_t + prev_h @ Wh
                i = jax.nn.sigmoid(a[:, :Hd])
                f = jax.nn.sigmoid(a[:, Hd:2 * Hd])
                o = jax.nn.sigmoid(a[:, 2 * Hd:3 * Hd])
                g = jnp.tanh(a[:, 3 * Hd:])
                next_c = f * prev_c + i * g
                next_h = o * jnp.tanh(next_c)
                return ((next_h, next_c), next_h)
            (_, _), hs = jax.lax.scan(step, (h0, c0), jnp.swapaxes(xW, 0, 1))
            return jnp.swapaxes(hs, 0, 1)
        return lstm_forward(x, h0, Wx, Wh, b)
    x = x + _L0_cond_ref(x, cond_1024, L0_cond_Wx, L0_cond_Wh, L0_cond_b)
    return x

_drawn_inputs = setup_inputs


def setup_inputs(seed=0):
    import zlib

    import numpy as np

    out = dict(_drawn_inputs(seed))
    spreads = {'L0_cond_b': (0.0, 0.1)}
    factors = {}
    for name, (base, spread) in spreads.items():
        noise = np.random.default_rng([zlib.crc32(name.encode()), seed]).standard_normal(out[name].shape)
        drawn = base * np.exp(spread * noise) if base else spread * noise
        out[name] = jnp.asarray(drawn.astype(out[name].dtype))
    for name, factor in factors.items():
        out[name] = (out[name] * factor).astype(out[name].dtype)
    return out
```

```python
import concourse.bass as bass
from concourse import mybir
from contextlib import ExitStack


def lstm_residual_kernel(nc, x, h0, wx, wh, b, out):
    fp32, fp16, i32 = mybir.dt.float32, mybir.dt.float16, mybir.dt.int32
    ALU = mybir.AluOpType
    ACT = mybir.ActivationFunctionType
    AX = mybir.AxisListType
    ds = bass.ds

    P = 128
    N, T, D = x.shape
    H = wh.shape[0]
    K = H // P
    GATES = 4
    TILES = GATES * H // P
    HALF_TILES = TILES // 2
    SL = K // 2
    ST = P // N
    BLOCKS = T // ST
    CHUNK_BLOCKS = 4
    CT = CHUNK_BLOCKS * ST
    CW = CT * N
    UNROLL = K
    GROUPS = ST // UNROLL
    RING = 2 * CT
    XRING = 16
    XT_RING = 2 * CHUNK_BLOCKS
    HRING = 4
    AHEAD = 2 * CHUNK_BLOCKS + 1
    FIRST_TILES = TILES + 1
    HB = SL * N
    assert K == 4 and D == H and ST * N == P and CW == 512 and XRING * 2 == BLOCKS

    H_EXP, TOP_EXP, LEAST = 14, 14, 2.0 ** -60
    ONE_EXPONENT = 1 << 23
    BIAS = 127
    WH, WX, X, H0 = range(4)

    def w_columns(half, g0, g1):
        return lambda w: w.rearrange("p k (g v c) -> p k g v c", g=GATES, v=2)[:, :, g0:g1, half, :]

    ctx = ExitStack()
    with ctx:
        def sb(name, shape, dt):
            return ctx.enter_context(nc.sbuf_tensor(name, shape, dt))

        def pb(name, shape, dt):
            return ctx.enter_context(nc.psum_tensor(name, shape, dt))

        def sem(name):
            return ctx.enter_context(nc.semaphore(name))

        wh_hi = sb("wh_hi", [P, K, TILES * P], fp16)
        wh_lo = sb("wh_lo", [P, K, TILES * P], fp16)
        wx_hi = sb("wx_hi", [P, K, TILES * P], fp16)
        wx_lo = sb("wx_lo", [P, K, TILES * P], fp16)
        proj = sb("proj", [P, RING, TILES, N], fp32)
        flat_proj = proj[:, :, :, :].rearrange("p t n b -> p (t n b)")
        wx_raw = flat_proj[:, 0:K * TILES * P].rearrange("p (k n) -> p k n", k=K)
        wh_raw = flat_proj[:, K * TILES * P:2 * K * TILES * P].rearrange("p (k n) -> p k n", k=K)
        x_rows = sb("x_rows", [P, XRING, D], fp32)
        x_stage = sb("x_stage", [P, D], fp32)
        xt_hi = sb("xt_hi", [P, K, XT_RING * P], fp16)
        xt_lo = sb("xt_lo", [P, K, XT_RING * P], fp16)
        h_hist = sb("h_hist", [P, HRING, K, P], fp32)
        h_stage = sb("h_stage", [P, K, P], fp32)
        out_rows = sb("out_rows", [P, 2, D], fp32)
        h_parts = [sb(f"h_parts{i}", [P, K, 2, N], fp16) for i in range(2)]
        gates = [sb(f"gates{v}", [P, (GATES + 1) * HB], fp32) for v in "ab"]
        summed = [sb(f"summed{v}", [P, GATES * HB], fp32) for v in "ab"]
        products = [sb(f"products{v}", [P, 2 * HB], fp32) for v in "ab"]
        o_scaled = [sb(f"o_scaled{v}", [P, HB], fp32) for v in "ab"]
        tanh_c = [sb(f"tanh_c{v}", [P, HB], fp32) for v in "ab"]
        ident = sb("ident", [P, P], fp32)
        ones = sb("ones", [GATES, P], fp32)
        b_rows = sb("b_rows", [TILES, P], fp32)
        b_scaled = sb("b_scaled", [P, TILES], fp32)
        h0_rows = sb("h0_rows", [N, H], fp32)
        h0_parts = sb("h0_parts", [P, K, 2, N], fp16)
        h0_sum = sb("h0_sum", [P, TILES, N], fp32)
        most = sb("most", [P, 4], fp32)
        most_x2 = sb("most_x2", [P, 2], fp32)
        top = sb("top", [4, 1], fp32)
        top_diag = sb("top_diag", [4, 4], fp32)
        power = sb("power", [P, 4], fp32)
        scale = sb("scale", [P, 4], fp32)
        half_scale = sb("half_scale", [P, 4], fp32)
        unit = sb("unit", [P, 1], fp32)
        bias_unit = sb("bias_unit", [P, 1], fp32)
        bias_unit_half = sb("bias_unit_half", [P, 1], fp32)
        proj_tmp = sb("proj_tmp", [P, 2], fp32)
        proj_unit = sb("proj_unit", [P, 1], fp32)
        h0_unit = sb("h0_unit", [P, 1], fp32)

        rec = [[pb(f"rec{v}{i}", [P, 512], fp32) for v in "ab"] for i in range(2)]
        p_proj = pb("p_proj", [P, CW], fp32)
        p_xt = pb("p_xt", [P, K * P], fp32)
        p_out = pb("p_out", [P, K * P], fp32)
        p_set = pb("p_set", [P, 512], fp32)
        BANK_USED = HALF_TILES * 2 * N

        def rec_tile(par, half, n):
            return rec[par][half][:, n * 2 * N:(n + 1) * 2 * N]

        s_wx_in = sem("wx_in")
        s_wh_in = sem("wh_in")
        s_small_in = sem("small_in")
        s_x_late = sem("x_late")
        s_x_in = sem("x_in")
        s_consts = sem("consts")
        s_small_t = sem("small_t")
        s_x_late_max = sem("x_late_max")
        s_most = sem("most_done")
        s_dve = sem("dve_setup")
        s_most_t = sem("most_t")
        s_top = sem("top_ready")
        s_power = sem("power_psum")
        s_scales = sem("scales_ready")
        s_wx_hi = sem("wx_hi_ready")
        s_wh_hi = sem("wh_hi_ready")
        s_wx_split = sem("wx_split")
        s_wh_split = sem("wh_split")
        s_h0_split = sem("h0_split")
        s_h0_prod = sem("h0_prod")
        s_h0_added = sem("h0_added")
        s_bank_set = sem("bank_bits_set")
        s_x_staged = sem("x_staged")
        s_xt_psum = sem("xt_psum")
        s_xt_hi = sem("xt_hi_ready")
        s_xt = sem("xt_ready")
        s_proj_psum = sem("proj_psum")
        s_proj = sem("proj_ready")
        s_seeded = sem("seeded")
        s_rec = [sem("rec_a"), sem("rec_b")]
        s_h = [sem("h_a"), sem("h_b")]
        s_summed = sem("summed_ready")
        s_gates = sem("gates_ready")
        s_products = sem("products_ready")
        s_cell = sem("cell_ready")
        s_o_scaled = sem("o_scaled_ready")
        s_tanh_c = sem("tanh_c_ready")
        s_h_made = sem("h_made")
        s_h_staged = sem("h_staged")
        s_out_psum = sem("out_psum")
        s_out_rows = sem("out_rows_ready")
        s_stored = sem("stored")

        PROJ, XT, OUT = 1, 2, 4
        xt_end = BLOCKS - AHEAD
        proj_end = BLOCKS - CHUNK_BLOCKS
        SEGMENTS = [(0, 1, PROJ | XT), (1, xt_end, PROJ | XT | OUT),
                    (xt_end, proj_end, PROJ | OUT), (proj_end, BLOCKS, OUT)]

        block = ctx.enter_context(nc.Block())

        @block.sync
        def _(sp):
            sp.dma_start(wx_raw, wx.rearrange("(k p) n -> p k n", p=P)).then_inc(s_wx_in, 16)
            sp.dma_start(b_rows[:, :], b.rearrange("(n c) -> n c", c=P)).then_inc(s_small_in, 16)
            sp.dma_start(h0_rows[:, :], h0).then_inc(s_small_in, 16)
            sp.dma_start(wh_raw, wh.rearrange("(k p) n -> p k n", p=P)).then_inc(s_wh_in, 16)
            for late in (1, 0):
                if not late:
                    sp.wait_ge(s_x_late_max, 1)
                for n in range(N):
                    half = x[n, late * XRING * ST:(late + 1) * XRING * ST, :]
                    d = sp.dma_start(x_rows[n * ST:(n + 1) * ST, :, :], half.rearrange("(s t) d -> t s d", t=ST))
                    d.then_inc(s_x_late, 16) if late else d.then_inc(s_x_in, 16 * 6)

            def store(blk):
                sp.wait_ge(s_out_rows, blk + 1)
                for n in range(N):
                    sp.dma_start(out[n, ds(blk * ST, ST), :],
                                 out_rows[n * ST:(n + 1) * ST, ds(blk % 2, 1), :].rearrange("p s d -> p (s d)")
                                 ).then_inc(s_stored, 16)

            with sp.Fori(0, XRING) as blk:
                store(blk)
                for n in range(N):
                    sp.dma_start(x_rows[n * ST:(n + 1) * ST, ds(blk % XRING, 1), :].rearrange("p s d -> p (s d)"),
                                 x[n, ds((blk + XRING) * ST, ST), :]).then_inc(s_x_in, 16)
            with sp.Fori(XRING, BLOCKS) as blk:
                store(blk)
            sp.wait_ge(s_stored, 16 * N * BLOCKS)

        @block.gpsimd
        def _(pool):
            nc.gpsimd.memset(ident[:, :], 0.0).then_inc(s_consts, 1)
            pool.wait_ge(s_consts, 1)
            nc.gpsimd.affine_select(out=ident[:, :], in_=ident[:, :], compare_op=ALU.not_equal, fill=1.0,
                                    base=0, pattern=[[-1, P]], channel_multiplier=1).then_inc(s_consts, 1)
            nc.gpsimd.memset(ones[:, :], 1.0).then_inc(s_consts, 1)

            def stage_x(blk, staged):
                nc.gpsimd.tensor_copy(x_stage[:, :], x_rows[:, ds(blk % XRING, 1), :].rearrange("p s d -> p (s d)")
                                      ).then_inc(s_x_staged, 1)

            pool.wait_ge(s_x_in, 16 * N * 6)
            with pool.Fori(0, AHEAD) as blk:
                pool.wait_ge(s_xt_psum, blk)
                stage_x(blk, blk)

            for first, end, parts in SEGMENTS:
                if not parts & (XT | OUT):
                    continue
                with pool.Fori(first, end) as blk:
                    if parts & XT:
                        pool.wait_ge(s_xt_psum, blk + AHEAD)
                        if first:
                            pool.wait_ge(s_x_in, 16 * N * blk)
                        stage_x(blk + AHEAD, blk + AHEAD)
                    if parts & OUT:
                        pool.wait_ge(s_h[0], blk * ST + 1)
                        pool.wait_ge(s_h[1], blk * ST + 1)
                        pool.wait_ge(s_out_psum, blk - 1)
                        nc.gpsimd.tensor_copy(h_stage[:, :, :].rearrange("p k c -> p (k c)"),
                                              h_hist[:, ds((blk + HRING - 1) % HRING, 1), :, :].rearrange("p s k c -> p (s k c)")
                                              ).then_inc(s_h_staged, 1)
            pool.wait_ge(s_h[0], T + 1)
            pool.wait_ge(s_h[1], T + 1)
            pool.wait_ge(s_out_psum, BLOCKS - 1)
            nc.gpsimd.tensor_copy(h_stage[:, :, :].rearrange("p k c -> p (k c)"),
                                  h_hist[:, (BLOCKS - 1) % HRING, :, :].rearrange("p k c -> p (k c)")
                                  ).then_inc(s_h_staged, 1)

        @block.tensor
        def _(pe):
            def transpose_x(count):
                pe.wait_ge(s_x_staged, count + 1)
                pe.wait_ge(s_xt, count)
                for k in range(K):
                    t = nc.tensor.transpose(p_xt[:, k * P:(k + 1) * P], x_stage[:, k * P:(k + 1) * P], ident[:, :])
                t.then_inc(s_xt_psum, 1)

            def transpose_h(count):
                pe.wait_ge(s_h_staged, count + 1)
                pe.wait_ge(s_out_rows, count)
                for k in range(K):
                    t = nc.tensor.transpose(p_out[:, k * P:(k + 1) * P], h_stage[:, k, :], ident[:, :])
                t.then_inc(s_out_psum, 1)

            def project(tile, k):
                if k == 0:
                    pe.wait_ge(s_proj, tile)
                w_col = ds((tile % TILES) * P, P)
                x_col = ds(((tile // TILES) % 2) * CW, CW)
                for i, (w, xt) in enumerate(((wx_hi, xt_hi), (wx_hi, xt_lo), (wx_lo, xt_hi))):
                    m = nc.tensor.matmul(p_proj[:, :], w[:, k, w_col], xt[:, k, x_col],
                                         start=(k == 0 and i == 0), stop=(k == K - 1 and i == 2))
                if k == K - 1:
                    m.then_inc(s_proj_psum, 1)

            def recur(par, half, tiles, ks, parts):
                for n in tiles:
                    for k in ks:
                        for w in (wh_hi, wh_lo):
                            m = nc.tensor.matmul(rec_tile(par, half, n),
                                                 w[:, k, (half * HALF_TILES + n) * P:(half * HALF_TILES + n + 1) * P],
                                                 parts[:, k, :, :].rearrange("p s b -> p (s b)"),
                                                 start=False, stop=True, skip_group_check=True)
                return m

            pe.wait_ge(s_consts, 3)
            pe.wait_ge(s_small_in, 32)
            nc.tensor.transpose(p_set[:, 0:TILES], b_rows[:, :], ident[0:TILES, 0:TILES])
            for k in range(K):
                t = nc.tensor.transpose(p_set[:, TILES + k * N:TILES + (k + 1) * N],
                                        h0_rows[:, k * P:(k + 1) * P], ident[0:N, 0:N])
            t.then_inc(s_small_t, 1)
            for par in range(2):
                for half in range(2):
                    m = nc.tensor.matmul(rec[par][half][:, 0:BANK_USED], ident[:, :], ident[:, 0:BANK_USED],
                                         start=True, stop=True)
            m.then_inc(s_bank_set, 1)
            pe.wait_ge(s_most, 1)
            nc.tensor.transpose(p_out[0:4, 0:P], most[:, :], ident[:, :]).then_inc(s_most_t, 1)
            pe.wait_ge(s_top, 1)
            nc.tensor.matmul(p_out[:, P:P + 4], ones[:, :], top_diag[:, :], start=True, stop=True).then_inc(s_power, 1)

            with pe.Fori(0, XT_RING) as blk:
                transpose_x(blk)
            pe.wait_ge(s_wx_split, 1)
            pe.wait_ge(s_xt, XT_RING)
            with pe.Fori(0, FIRST_TILES) as tile:
                for k in range(K):
                    project(tile, k)
            transpose_x(XT_RING)
            pe.wait_ge(s_wh_split, 1)
            pe.wait_ge(s_h0_split, 1)
            for n in range(TILES):
                for k in range(K):
                    for i, w in enumerate((wh_hi, wh_lo)):
                        m = nc.tensor.matmul(p_set[:, n * 2 * N:(n + 1) * 2 * N], w[:, k, n * P:(n + 1) * P],
                                             h0_parts[:, k, :, :].rearrange("p s b -> p (s b)"),
                                             start=(k == 0 and i == 0), stop=(k == K - 1 and i == 1))
            m.then_inc(s_h0_prod, 1)

            low, high = range(0, K // 2), range(K // 2, K)
            every, first_b, last_b = range(HALF_TILES), range(HALF_TILES // 2), range(HALF_TILES // 2, HALF_TILES)
            for first, end, parts in SEGMENTS:
                with pe.Fori(first, end) as blk:
                    with pe.Fori(0, GROUPS) as group:
                        step0 = pe.snap(blk * ST + group * UNROLL)
                        for u in range(UNROLL):
                            par, h_in = u % 2, h_parts[(u + 1) % 2]
                            pe.wait_ge(s_seeded, step0 + u + 1)
                            pe.wait_ge(s_h[0], step0 + u + 1)
                            recur(par, 0, every, low, h_in)
                            recur(par, 1, first_b, low, h_in)
                            pe.wait_ge(s_h[1], step0 + u + 1)
                            recur(par, 0, every, high, h_in).then_inc(s_rec[0], 1)
                            recur(par, 1, last_b, low, h_in)
                            recur(par, 1, every, high, h_in).then_inc(s_rec[1], 1)
                            if parts & PROJ:
                                if u == 0 and parts & XT:
                                    pe.wait_ge(s_xt, ((blk * GROUPS + group + FIRST_TILES) // TILES + 1) * CHUNK_BLOCKS)
                                if u == 0 and not parts & XT:
                                    pe.wait_ge(s_xt, BLOCKS)
                                project(blk * GROUPS + group + FIRST_TILES, u)
                    if parts & XT:
                        transpose_x(blk + AHEAD)
                    if parts & OUT:
                        transpose_h(blk - 1)
            transpose_h(BLOCKS - 1)

        @block.scalar
        def _(act):
            def high_parts(raw, hi, which, done):
                for half in range(2):
                    tiles = hi[:, :, half * HALF_TILES * P:(half + 1) * HALF_TILES * P].rearrange("p k (g c) -> p k g c", g=GATES)
                    for g0, g1, by in ((0, 3, half_scale), (3, 4, scale)):
                        for k in range(K):
                            a = nc.scalar.activation(tiles[:, k, g0:g1, :], w_columns(half, g0, g1)(raw)[:, k, :, :],
                                                     ACT.Copy, scale=by[:, which:which + 1])
                a.then_inc(done, 1)

            def x_high(count):
                act.wait_ge(s_xt_psum, count + 1)
                nc.scalar.activation(xt_hi[:, :, ds((count % XT_RING) * P, P)],
                                     p_xt[:, :].rearrange("p (k c) -> p k c", k=K),
                                     ACT.Copy, scale=scale[:, X:X + 1]).then_inc(s_xt_hi, 1)

            def keep_projection(tile):
                act.wait_ge(s_proj_psum, tile + 1)
                to = proj[:, ds(((tile // TILES) % 2) * CT, CT), ds(tile % TILES, 1), :]
                nc.scalar.activation(to.rearrange("p (q t) n b -> p q t (n b)", t=ST),
                                     p_proj[:, :].rearrange("p (q b t) -> p q t b", b=N, t=ST),
                                     ACT.Identity, scale=proj_unit[:, 0:1],
                                     bias=b_scaled[:, ds(tile % TILES, 1)]).then_inc(s_proj, 1)

            def seed(step, par):
                for half in range(2):
                    a = nc.scalar.activation(
                        rec[par][half][:, 0:BANK_USED].rearrange("p (n s b) -> p n s b", s=2, b=N),
                        proj[:, ds(step % RING, 1), half * HALF_TILES:(half + 1) * HALF_TILES, :].rearrange("p t n b -> p (t n) b")
                        .unsqueeze(2).broadcast_to([P, HALF_TILES, 2, N]),
                        ACT.Copy)
                a.then_inc(s_seeded, 1)

            act.wait_ge(s_scales, 1)
            act.wait_ge(s_wx_in, 16)
            high_parts(wx_raw, wx_hi, WX, s_wx_hi)
            act.wait_ge(s_wh_in, 16)
            high_parts(wh_raw, wh_hi, WH, s_wh_hi)
            with act.Fori(0, XT_RING) as blk:
                x_high(blk)
            act.wait_ge(s_wx_split, 1)
            act.wait_ge(s_wh_split, 1)
            with act.Fori(0, FIRST_TILES) as tile:
                keep_projection(tile)
            x_high(XT_RING)
            act.wait_ge(s_bank_set, 1)
            act.wait_ge(s_h0_added, 1)
            seed(0, 0)

            for first, end, parts in SEGMENTS:
                with act.Fori(first, end) as blk:
                    with act.Fori(0, GROUPS) as group:
                        step0 = act.snap(blk * ST + group * UNROLL)
                        for u in range(UNROLL):
                            if u == UNROLL - 1 and parts & PROJ:
                                act.wait_ge(s_proj, ((step0 + UNROLL) // CT + 1) * TILES)
                            seed(step0 + u + 1, (u + 1) % 2)
                            for half in range(2):
                                turn = step0 * 2 + (2 * u + half + 1)
                                act.wait_ge(s_summed, turn)
                                nc.scalar.activation(gates[half][:, 0:GATES * HB], summed[half][:, :], ACT.Tanh,
                                                     scale=unit[:, 0:1]).then_inc(s_gates, 1)
                                act.wait_ge(s_cell, turn)
                                nc.scalar.activation(tanh_c[half][:, :], gates[half][:, GATES * HB:], ACT.Tanh,
                                                     scale=0.5).then_inc(s_tanh_c, 1)
                        if parts & PROJ:
                            keep_projection(blk * GROUPS + group + FIRST_TILES)
                    if parts & XT:
                        x_high(blk + AHEAD)

        @block.vector
        def _(dve):
            chained = [0]

            def chain(instruction):
                chained[0] += 1
                instruction.then_inc(s_dve, 1)
                dve.wait_ge(s_dve, chained[0])

            def low_parts(raw, hi, lo, which, high_done, done):
                dve.wait_ge(high_done, 1)
                for half in range(2):
                    cut = [w[:, :, half * HALF_TILES * P:(half + 1) * HALF_TILES * P].rearrange("p k (g c) -> p k g c", g=GATES)
                           for w in (hi, lo)]
                    for g0, g1, by in ((0, 3, half_scale), (3, 4, scale)):
                        for k in range(K):
                            i = nc.vector.scalar_tensor_tensor(cut[1][:, k, g0:g1, :], w_columns(half, g0, g1)(raw)[:, k, :, :],
                                                               by[:, which:which + 1], cut[0][:, k, g0:g1, :],
                                                               ALU.mult, ALU.subtract)
                i.then_inc(done, 1)

            def x_low(count):
                dve.wait_ge(s_xt_hi, count + 1)
                nc.vector.scalar_tensor_tensor(xt_lo[:, :, ds((count % XT_RING) * P, P)],
                                               p_xt[:, :].rearrange("p (k c) -> p k c", k=K), scale[:, X:X + 1],
                                               xt_hi[:, :, ds((count % XT_RING) * P, P)],
                                               ALU.mult, ALU.subtract).then_inc(s_xt, 1)

            def add_x(blk):
                dve.wait_ge(s_out_psum, blk + 1)
                nc.vector.scalar_tensor_tensor(out_rows[:, ds(blk % 2, 1), :].rearrange("p s d -> p (s d)"), p_out[:, :],
                                               2.0 ** -H_EXP, x_rows[:, ds(blk % XRING, 1), :].rearrange("p s d -> p (s d)"),
                                               ALU.mult, ALU.add).then_inc(s_out_rows, 1)

            for half in range(2):
                nc.vector.memset(gates[half][:, GATES * HB:], 0.0)
            for half in range(2):
                nc.vector.memset(h_parts[1][:, half * SL:(half + 1) * SL, :, :], 0.0).then_inc(s_h[half], 1)

            def most_of(to, of, axis):
                return nc.vector.tensor_reduce(to, of, axis=axis, op=ALU.max, apply_absolute_value=True)

            dve.wait_ge(s_wx_in, 16)
            most_of(most[:, WX:WX + 1], wx_raw, AX.XY)
            dve.wait_ge(s_wh_in, 16)
            most_of(most[:, WH:WH + 1], wh_raw, AX.XY)
            dve.wait_ge(s_small_t, 1)
            most_of(most[:, H0:H0 + 1], p_set[:, TILES:TILES + K * N], AX.X)
            dve.wait_ge(s_x_late, 16 * N)
            most_of(most_x2[:, 1:2], x_rows[:, :, :], AX.XY).then_inc(s_x_late_max, 1)
            dve.wait_ge(s_x_in, 16 * N * 6)
            chain(most_of(most_x2[:, 0:1], x_rows[:, :, :], AX.XY))
            dve.wait_ge(s_x_late_max, 1)
            nc.vector.tensor_reduce(most[:, X:X + 1], most_x2[:, :], axis=AX.X, op=ALU.max).then_inc(s_most, 1)
            dve.wait_ge(s_most_t, 1)
            chain(nc.vector.tensor_reduce(top[:, :], p_out[0:4, 0:P], axis=AX.X, op=ALU.max))
            chain(nc.vector.tensor_scalar(top[:, :], top[:, :], LEAST, None, ALU.max))
            chain(nc.vector.tensor_scalar(top[:, :].bitcast(i32), top[:, :].bitcast(i32), (255 << 23), None, ALU.bitwise_and))
            nc.vector.tensor_scalar(top_diag[:, :], ident[0:4, 0:4], top[:, 0:1], None, ALU.mult).then_inc(s_top, 1)
            dve.wait_ge(s_power, 1)
            chain(nc.vector.tensor_copy(power[:, :], p_out[:, P:P + 4]))
            chain(nc.vector.tensor_scalar(scale[:, :].bitcast(i32), power[:, :].bitcast(i32), -1.0,
                                          float((2 * BIAS + TOP_EXP) * ONE_EXPONENT), ALU.mult, ALU.add))
            nc.vector.tensor_scalar(half_scale[:, :], scale[:, :], 0.5, None, ALU.mult)
            nc.vector.tensor_scalar(unit[:, :], power[:, WH:WH + 1], 2.0 ** -(TOP_EXP + H_EXP), None, ALU.mult)
            chain(nc.vector.tensor_scalar(bias_unit[:, :], scale[:, WH:WH + 1], 2.0 ** (H_EXP - 1), None, ALU.mult))
            nc.vector.tensor_scalar(bias_unit_half[:, :], bias_unit[:, :], 0.5, None, ALU.mult)
            nc.vector.tensor_scalar(h0_unit[:, :], power[:, H0:H0 + 1], 2.0 ** (H_EXP - 1 - TOP_EXP), None, ALU.mult)
            chain(nc.vector.tensor_scalar(proj_tmp[:, 0:1], bias_unit[:, :], 2.0 ** (-2 * TOP_EXP), None, ALU.mult))
            chain(nc.vector.tensor_tensor(proj_tmp[:, 1:2], proj_tmp[:, 0:1], power[:, X:X + 1], ALU.mult))
            chain(nc.vector.tensor_tensor(proj_unit[:, :], proj_tmp[:, 1:2], power[:, WX:WX + 1], ALU.mult))
            for half in range(2):
                b_t = p_set[:, 0:TILES].rearrange("p (g v s) -> p g v s", g=GATES, v=2)[:, :, half, :]
                to = b_scaled[:, half * HALF_TILES:(half + 1) * HALF_TILES].rearrange("p (g s) -> p g s", g=GATES)
                nc.vector.tensor_scalar(to[:, 0:3, :], b_t[:, 0:3, :], bias_unit_half[:, 0:1], None, ALU.mult)
                nc.vector.tensor_scalar(to[:, 3:4, :], b_t[:, 3:4, :], bias_unit[:, 0:1], None, ALU.mult)
            h0_t = p_set[:, TILES:TILES + K * N].rearrange("p (k b) -> p k b", k=K)
            chain(nc.vector.tensor_scalar(h0_parts[:, :, 0, :], h0_t, scale[:, H0:H0 + 1], None, ALU.mult))
            nc.vector.scalar_tensor_tensor(h0_parts[:, :, 1, :], h0_t, scale[:, H0:H0 + 1], h0_parts[:, :, 0, :],
                                           ALU.mult, ALU.subtract).then_inc(s_h0_split, 1)
            nc.vector.tensor_copy(proj_tmp[:, 0:1], proj_tmp[:, 1:2]).then_inc(s_scales, 1)
            low_parts(wx_raw, wx_hi, wx_lo, WX, s_wx_hi, s_wx_split)
            low_parts(wh_raw, wh_hi, wh_lo, WH, s_wh_hi, s_wh_split)
            with dve.Fori(0, XT_RING) as blk:
                x_low(blk)
            dve.wait_ge(s_h0_prod, 1)
            chain(nc.vector.tensor_reduce(h0_sum[:, :, :], p_set[:, 0:TILES * 2 * N].rearrange("p (n s b) -> p n b s", s=2, b=N),
                                          axis=AX.X, op=ALU.add))
            dve.wait_ge(s_proj, FIRST_TILES)
            nc.vector.scalar_tensor_tensor(proj[:, 0, :, :], h0_sum[:, :, :], h0_unit[:, 0:1], proj[:, 0, :, :],
                                           ALU.mult, ALU.add).then_inc(s_h0_added, 1)
            x_low(XT_RING)

            for first, end, parts in SEGMENTS:
                with dve.Fori(first, end) as blk:
                    with dve.Fori(0, GROUPS) as group:
                        step0 = dve.snap(blk * ST + group * UNROLL)
                        for u in range(UNROLL):
                            for half in range(2):
                                turn = step0 * 2 + (2 * u + half + 1)
                                s0 = half * SL
                                gate = gates[half]
                                h_out = h_parts[u % 2]
                                dve.wait_ge(s_rec[half], step0 + u + 1)
                                nc.vector.tensor_reduce(summed[half][:, :].rearrange("p (n b) -> p n b", b=N),
                                                        rec[u % 2][half][:, 0:BANK_USED].rearrange("p (n s b) -> p n b s", s=2, b=N),
                                                        axis=AX.X, op=ALU.add).then_inc(s_summed, 1)
                                dve.wait_ge(s_gates, turn)
                                nc.vector.scalar_tensor_tensor(products[half][:, :], gate[:, 0:2 * HB], 1.0, gate[:, 3 * HB:5 * HB],
                                                               ALU.add, ALU.mult).then_inc(s_products, 1)
                                dve.wait_ge(s_products, turn)
                                nc.vector.scalar_tensor_tensor(gate[:, 4 * HB:5 * HB], products[half][:, HB:2 * HB], 0.5,
                                                               products[half][:, 0:HB], ALU.mult, ALU.add).then_inc(s_cell, 1)
                                nc.vector.tensor_scalar(o_scaled[half][:, :], gate[:, 2 * HB:3 * HB], 1.0, 2.0 ** (H_EXP - 1),
                                                        ALU.add, ALU.mult).then_inc(s_o_scaled, 1)
                                dve.wait_ge(s_o_scaled, turn)
                                dve.wait_ge(s_tanh_c, turn)
                                o3 = o_scaled[half][:, :].rearrange("p (s b) -> p s b", s=SL)
                                tc3 = tanh_c[half][:, :].rearrange("p (s b) -> p s b", s=SL)
                                hist = h_hist[:, ds(blk % HRING, 1), s0:s0 + SL, :].rearrange("p r s (b t) -> p (r s) b t", t=ST)
                                hist = hist[:, :, :, ds(group * UNROLL + u, 1)].rearrange("p s b t -> p s (b t)")
                                nc.vector.tensor_tensor(hist, o3, tc3, ALU.mult).then_inc(s_h_made, 1)
                                nc.vector.tensor_tensor(h_out[:, s0:s0 + SL, 0, :], o3, tc3, ALU.mult).then_inc(s_h_made, 1)
                                dve.wait_ge(s_h_made, turn * 2)
                                nc.vector.tensor_tensor(h_out[:, s0:s0 + SL, 1, :], hist, h_out[:, s0:s0 + SL, 0, :],
                                                        ALU.subtract).then_inc(s_h[half], 1)
                    if parts & XT:
                        x_low(blk + AHEAD)
                    if parts & OUT:
                        dve.wait_ge(s_stored, 16 * N * (blk - 1))
                        add_x(blk - 1)
            dve.wait_ge(s_stored, 16 * N * (BLOCKS - 1))
            add_x(BLOCKS - 1)


_INS = ["x", "cond_1024", "L0_cond_Wx", "L0_cond_Wh", "L0_cond_b"]
_OUTS = [((8, 512, 512), "float32")]


def kernel(**inputs):
    import numpy as _np
    import concourse.bacc as _bacc
    from concourse import mybir as _mybir
    from concourse.bass_utils import run_bass_kernel_spmd as _run

    nc = _bacc.Bacc("TRN2", target_bir_lowering=False, num_devices=1)
    arrays, args = {}, []
    for name in _INS:
        a = _np.ascontiguousarray(inputs[name])
        arrays[f"in_{name}_dram"] = a
        args.append(nc.dram_tensor(f"in_{name}_dram", a.shape, _mybir.dt.from_np(a.dtype), kind="ExternalInput").ap())
    for i, (shape, dtype) in enumerate(_OUTS):
        dt = _mybir.dt.from_np(_np.dtype(dtype))
        args.append(nc.dram_tensor(f"out_{i}_dram", shape, dt, kind="ExternalOutput").ap())
    lstm_residual_kernel(nc, *args)
    r = _run(nc, [arrays], core_ids=[0])
    got = tuple(r.results[0][f"out_{i}_dram"] for i in range(len(_OUTS)))
    return got[0]
```

```python
import concourse.bass as bass
from concourse import mybir
from contextlib import ExitStack


def lstm_residual_kernel(nc, x, h0, wx, wh, b, out):
    fp32, fp16, i32 = mybir.dt.float32, mybir.dt.float16, mybir.dt.int32
    ALU = mybir.AluOpType
    ACT = mybir.ActivationFunctionType
    AX = mybir.AxisListType
    ds = bass.ds

    P = 128
    N, T, D = x.shape
    H = wh.shape[0]
    K = H // P
    GATES = 4
    TILES = GATES * H // P
    HALF_TILES = TILES // 2
    SL = K // 2
    ST = P // N
    BLOCKS = T // ST
    CHUNK_BLOCKS = 4
    CT = CHUNK_BLOCKS * ST
    CW = CT * N
    UNROLL = K
    GROUPS = ST // UNROLL
    RING = 2 * CT
    XRING = 16
    XT_RING = 2 * CHUNK_BLOCKS
    HRING = 4
    AHEAD = 2 * CHUNK_BLOCKS + 1
    FIRST_TILES = TILES + 1
    HB = SL * N
    COLS = 2 * 2 * N
    assert K == 4 and D == H and ST * N == P and CW == 512 and XRING * 2 == BLOCKS

    H_EXP, TOP_EXP, LEAST = 14, 14, 2.0 ** -60
    ONE_EXPONENT = 1 << 23
    BIAS = 127
    WH, WX, X, H0 = range(4)

    def w_columns(half, g0, g1):
        return lambda w: w.rearrange("p k (g v c) -> p k g v c", g=GATES, v=2)[:, :, g0:g1, half, :]

    def half_columns(w, half):
        return w[:, :, half * HALF_TILES * P:(half + 1) * HALF_TILES * P].rearrange("p k (g c) -> p k g c", g=GATES)

    ctx = ExitStack()
    with ctx:
        def sb(name, shape, dt):
            return ctx.enter_context(nc.sbuf_tensor(name, shape, dt))

        def pb(name, shape, dt):
            return ctx.enter_context(nc.psum_tensor(name, shape, dt))

        def sem(name):
            return ctx.enter_context(nc.semaphore(name))

        wh_parts = sb("wh_parts", [P, 2, K, TILES * P], fp16)
        wh_hi, wh_lo = wh_parts[:, 0, :, :], wh_parts[:, 1, :, :]
        x_late = wh_parts[:, :, :, :].rearrange("p s k n -> p (s k n)").bitcast(fp32).rearrange("p (s d) -> p s d", d=D)
        wx_hi = sb("wx_hi", [P, K, TILES * P], fp16)
        wx_lo = sb("wx_lo", [P, K, TILES * P], fp16)
        proj = sb("proj", [P, RING, TILES, N], fp32)
        flat_proj = proj[:, :, :, :].rearrange("p t n b -> p (t n b)")
        wx_raw = flat_proj[:, 0:K * TILES * P].rearrange("p (k n) -> p k n", k=K)
        wh_raw = flat_proj[:, K * TILES * P:2 * K * TILES * P].rearrange("p (k n) -> p k n", k=K)
        x_rows = sb("x_rows", [P, XRING, D], fp32)
        x_stage = sb("x_stage", [P, D], fp32)
        xt_hi = sb("xt_hi", [P, K, XT_RING * P], fp16)
        xt_lo = sb("xt_lo", [P, K, XT_RING * P], fp16)
        h_hist = sb("h_hist", [P, HRING * ST, K, N], fp32)
        h_now = [sb(f"h_now{u}", [P, K, N], fp32) for u in range(UNROLL)]
        h_stage = sb("h_stage", [P, K, P], fp32)
        out_rows = sb("out_rows", [P, 2, D], fp32)
        h_parts = [sb(f"h_parts{i}", [P, K, 2, N], fp16) for i in range(2)]
        gates = [sb(f"gates{v}", [P, (GATES + 1) * HB], fp32) for v in "ab"]
        summed = [sb(f"summed{v}", [P, GATES * HB], fp32) for v in "ab"]
        products = [sb(f"products{v}", [P, 2 * HB], fp32) for v in "ab"]
        o_scaled = [sb(f"o_scaled{v}", [P, HB], fp32) for v in "ab"]
        tanh_c = [sb(f"tanh_c{v}", [P, HB], fp32) for v in "ab"]
        ident = sb("ident", [P, P], fp32)
        ones = sb("ones", [GATES, P], fp32)
        b_rows = sb("b_rows", [TILES, P], fp32)
        b_scaled = sb("b_scaled", [P, TILES], fp32)
        h0_rows = sb("h0_rows", [N, H], fp32)
        h0_parts = sb("h0_parts", [P, K, 2, N], fp16)
        h0_sum = sb("h0_sum", [P, TILES, N], fp32)
        most = sb("most", [P, 4], fp32)
        most_parts = sb("most_parts", [P, 2 + 2 * K], fp32)
        top = sb("top", [4, 1], fp32)
        top_diag = sb("top_diag", [4, 4], fp32)
        power = sb("power", [P, 4], fp32)
        scale = sb("scale", [P, 4], fp32)
        half_scale = sb("half_scale", [P, 4], fp32)
        unit = sb("unit", [P, 1], fp32)
        bias_unit = sb("bias_unit", [P, 1], fp32)
        bias_unit_half = sb("bias_unit_half", [P, 1], fp32)
        proj_tmp = sb("proj_tmp", [P, 2], fp32)
        proj_unit = sb("proj_unit", [P, 1], fp32)
        h0_unit = sb("h0_unit", [P, 1], fp32)

        rec = [pb(f"rec{i}", [P, 2, 512], fp32) for i in range(2)]
        p_proj = pb("p_proj", [P, CW], fp32)
        p_xt = pb("p_xt", [P, K * P], fp32)
        p_out = pb("p_out", [P, K * P], fp32)
        p_set = pb("p_set", [P, 512], fp32)

        def rec_tile(par, half, n):
            return rec[par][:, half, n * COLS:(n + 1) * COLS]

        def rec_parts(par, half):
            return rec[par][:, half, 0:HALF_TILES * COLS].rearrange("p (n s b) -> p n s b", s=COLS // N, b=N)[:, :, 0:2, :]

        XT_BANKS = (p_xt, p_out)
        PROJ_BANKS = (p_proj, p_out)

        s_wx_in = [sem(f"wx_in{k}") for k in range(K)]
        s_wh_in = [sem(f"wh_in{k}") for k in range(K)]
        s_small_in = sem("small_in")
        s_x_late = sem("x_late")
        s_x_in = sem("x_in")
        s_consts = sem("consts")
        s_small_t = sem("small_t")
        s_most = sem("most_done")
        s_dve = sem("dve_setup")
        s_most_t = sem("most_t")
        s_top = sem("top_ready")
        s_power = sem("power_psum")
        s_scales = sem("scales_ready")
        s_wx_hi = sem("wx_hi_ready")
        s_wh_hi = sem("wh_hi_ready")
        s_wx_split = sem("wx_split")
        s_wh_split = sem("wh_split")
        s_h0_prod = sem("h0_prod")
        s_h0_added = sem("h0_added")
        s_bank_set = sem("bank_bits_set")
        s_x_staged = sem("x_staged")
        s_xt_psum = sem("xt_psum")
        s_xt_hi = sem("xt_hi_ready")
        s_xt = sem("xt_ready")
        s_proj_psum = sem("proj_psum")
        s_proj = sem("proj_ready")
        s_seeded = sem("seeded")
        s_rec = [sem("rec_a"), sem("rec_b")]
        s_h = [sem("h_a"), sem("h_b")]
        s_summed = sem("summed_ready")
        s_gates = sem("gates_ready")
        s_products = sem("products_ready")
        s_cell = sem("cell_ready")
        s_tanh_c = sem("tanh_c_ready")
        s_h_made = sem("h_made")
        s_h_last = sem("h_last_kept")
        s_h_staged = sem("h_staged")
        s_out_psum = sem("out_psum")
        s_out_rows = sem("out_rows_ready")
        s_stored = sem("stored")

        PROJ, XT, OUT = 1, 2, 4
        xt_end = BLOCKS - AHEAD
        proj_end = BLOCKS - CHUNK_BLOCKS
        SEGMENTS = [(0, 1, PROJ | XT), (1, xt_end, PROJ | XT | OUT),
                    (xt_end, proj_end, PROJ | OUT), (proj_end, BLOCKS, OUT)]

        block = ctx.enter_context(nc.Block())

        @block.sync
        def _(sp):
            for k in range(K):
                sp.dma_start(wx_raw[:, k, :], wx[k * P:(k + 1) * P, :]).then_inc(s_wx_in[k], 16)
            sp.dma_start(b_rows[:, :], b.rearrange("(n c) -> n c", c=P)).then_inc(s_small_in, 16)
            sp.dma_start(h0_rows[:, :], h0).then_inc(s_small_in, 16)
            for n in range(N):
                sp.dma_start(x_late[n * ST:(n + 1) * ST, :, :],
                             x[n, XRING * ST:, :].rearrange("(s t) d -> t s d", t=ST)).then_inc(s_x_late, 16)
            for n in range(N):
                sp.dma_start(x_rows[n * ST:(n + 1) * ST, :, :],
                             x[n, 0:XRING * ST, :].rearrange("(s t) d -> t s d", t=ST)).then_inc(s_x_in, 16 * 6)
            for k in range(K):
                sp.dma_start(wh_raw[:, k, :], wh[k * P:(k + 1) * P, :]).then_inc(s_wh_in[k], 16)

            def store(blk):
                sp.wait_ge(s_out_rows, blk + 1)
                for n in range(N):
                    sp.dma_start(out[n, ds(blk * ST, ST), :],
                                 out_rows[n * ST:(n + 1) * ST, ds(blk % 2, 1), :].rearrange("p s d -> p (s d)")
                                 ).then_inc(s_stored, 16)

            with sp.Fori(0, XRING) as blk:
                store(blk)
                for n in range(N):
                    sp.dma_start(x_rows[n * ST:(n + 1) * ST, ds(blk % XRING, 1), :].rearrange("p s d -> p (s d)"),
                                 x[n, ds((blk + XRING) * ST, ST), :]).then_inc(s_x_in, 16)
            with sp.Fori(XRING, BLOCKS) as blk:
                store(blk)
            sp.wait_ge(s_stored, 16 * N * BLOCKS)

        @block.gpsimd
        def _(pool):
            nc.gpsimd.memset(ident[:, :], 0.0).then_inc(s_consts, 1)
            pool.wait_ge(s_consts, 1)
            nc.gpsimd.affine_select(out=ident[:, :], in_=ident[:, :], compare_op=ALU.not_equal, fill=1.0,
                                    base=0, pattern=[[-1, P]], channel_multiplier=1).then_inc(s_consts, 1)
            nc.gpsimd.memset(ones[:, :], 1.0).then_inc(s_consts, 1)

            def stage_x(blk):
                nc.gpsimd.tensor_copy(x_stage[:, :], x_rows[:, ds(blk % XRING, 1), :].rearrange("p s d -> p (s d)")
                                      ).then_inc(s_x_staged, 1)

            def stage_h(at):
                nc.gpsimd.tensor_copy(h_stage[:, :, :].rearrange("p k (b t) -> p k b t", t=ST),
                                      h_hist[:, ds(at, ST), :, :].rearrange("p t k b -> p k b t")).then_inc(s_h_staged, 1)

            pool.wait_ge(s_scales, 1)
            for half in range(2):
                tiles = half_columns(wh_hi, half)
                for g0, g1, by in ((0, 3, half_scale), (3, 4, scale)):
                    for k in range(K):
                        i = nc.gpsimd.tensor_scalar(tiles[:, k, g0:g1, :], w_columns(half, g0, g1)(wh_raw)[:, k, :, :],
                                                    by[:, WH:WH + 1], None, ALU.mult)
            i.then_inc(s_wh_hi, 1)
            stage_x(XT_RING)

            for first, end, parts in SEGMENTS:
                if not parts & (XT | OUT):
                    continue
                with pool.Fori(first, end) as blk:
                    if parts & XT:
                        pool.wait_ge(s_xt_psum, blk + AHEAD)
                        if first:
                            pool.wait_ge(s_x_in, 16 * N * blk)
                        stage_x(blk + AHEAD)
                    if parts & OUT:
                        pool.wait_ge(s_tanh_c, blk * ST * 2 + 1)
                        pool.wait_ge(s_out_psum, blk - 1)
                        stage_h(((blk + HRING - 1) % HRING) * ST)
            pool.wait_ge(s_h_last, 1)
            pool.wait_ge(s_out_psum, BLOCKS - 1)
            stage_h((BLOCKS - 1) % HRING * ST)

        @block.tensor
        def _(pe):
            def transpose_x(bank, rows):
                for k in range(K):
                    t = nc.tensor.transpose(bank[:, k * P:(k + 1) * P], rows[:, k * P:(k + 1) * P], ident[:, :])
                t.then_inc(s_xt_psum, 1)

            def transpose_staged_x(blk):
                pe.wait_ge(s_x_staged, blk - XT_RING + 1)
                pe.wait_ge(s_xt, blk)
                transpose_x(p_xt, x_stage)

            def transpose_h(count):
                pe.wait_ge(s_h_staged, count + 1)
                pe.wait_ge(s_out_rows, count)
                for k in range(K):
                    t = nc.tensor.transpose(p_out[:, k * P:(k + 1) * P], h_stage[:, k, :], ident[:, :])
                t.then_inc(s_out_psum, 1)

            def project(tile, k, bank=p_proj):
                w_col = ds((tile % TILES) * P, P)
                x_col = ds(((tile // TILES) % 2) * CW, CW)
                for i, (w, xt) in enumerate(((wx_hi, xt_hi), (wx_hi, xt_lo), (wx_lo, xt_hi))):
                    m = nc.tensor.matmul(bank[:, :], w[:, k, w_col], xt[:, k, x_col],
                                         start=(k == 0 and i == 0), stop=(k == K - 1 and i == 2))
                if k == K - 1:
                    m.then_inc(s_proj_psum, 1)

            def recur(par, half, tiles, ks, parts):
                for n in tiles:
                    for k in ks:
                        for w in (wh_hi, wh_lo):
                            m = nc.tensor.matmul(rec_tile(par, half, n),
                                                 w[:, k, (half * HALF_TILES + n) * P:(half * HALF_TILES + n + 1) * P],
                                                 parts[:, k, :, :].rearrange("p s b -> p (s b)")
                                                 .unsqueeze(1).broadcast_to([P, COLS // (2 * N), 2 * N]),
                                                 start=False, stop=True, skip_group_check=True)
                return m

            pe.wait_ge(s_consts, 3)
            pe.wait_ge(s_small_in, 32)
            nc.tensor.transpose(p_set[:, 0:TILES], b_rows[:, :], ident[0:TILES, 0:TILES])
            for k in range(K):
                t = nc.tensor.transpose(p_set[:, TILES + k * N:TILES + (k + 1) * N],
                                        h0_rows[:, k * P:(k + 1) * P], ident[0:N, 0:N])
            t.then_inc(s_small_t, 1)
            for par in range(2):
                for half in range(2):
                    for n in range(2):
                        m = nc.tensor.matmul(rec[par][:, half, n * P:(n + 1) * P], ident[:, :], ident[:, :],
                                             start=(n == 0), stop=True, skip_group_check=True)
            m.then_inc(s_bank_set, 1)
            pe.wait_ge(s_most, 1)
            nc.tensor.transpose(p_out[0:4, 0:P], most[:, :], ident[:, :]).then_inc(s_most_t, 1)
            pe.wait_ge(s_top, 1)
            nc.tensor.matmul(p_out[:, P:P + 4], ones[:, :], top_diag[:, :], start=True, stop=True).then_inc(s_power, 1)

            pe.wait_ge(s_x_in, 16 * N * 6)
            for blk in range(XT_RING):
                pe.wait_ge(s_scales, 1) if blk < 2 else pe.wait_ge(s_xt, blk - 1)
                transpose_x(XT_BANKS[blk % 2], x_rows[:, blk, :])

            def project_tile(tile, i):
                for k in range(K):
                    project(tile, k, PROJ_BANKS[i])

            pe.wait_ge(s_xt, XT_RING)
            pe.wait_ge(s_wx_split, 1)
            for i in range(2):
                project_tile(i, i)
            with pe.Fori(1, HALF_TILES // 2) as pair:
                for i in range(2):
                    pe.wait_ge(s_proj, pair * 2 + i - 1)
                    project_tile(pair * 2 + i, i)
            pe.wait_ge(s_wx_split, 2)
            with pe.Fori(HALF_TILES // 2, TILES // 2 - 1) as pair:
                for i in range(2):
                    pe.wait_ge(s_proj, pair * 2 + i - 1)
                    project_tile(pair * 2 + i, i)
            pe.wait_ge(s_wh_split, 1)
            for n in range(TILES):
                for k in range(K):
                    for i, w in enumerate((wh_hi, wh_lo)):
                        m = nc.tensor.matmul(p_set[:, n * 2 * N:(n + 1) * 2 * N], w[:, k, n * P:(n + 1) * P],
                                             h0_parts[:, k, :, :].rearrange("p s b -> p (s b)"),
                                             start=(k == 0 and i == 0), stop=(k == K - 1 and i == 1))
            m.then_inc(s_h0_prod, 1)
            for tile in range(TILES - 2, TILES + 1):
                pe.wait_ge(s_proj, tile - 1)
                project_tile(tile, tile % 2)
            transpose_staged_x(XT_RING)
            pe.wait_ge(s_seeded, 1)

            low, high = range(0, K // 2), range(K // 2, K)
            every, first_b, last_b = range(HALF_TILES), range(HALF_TILES // 2), range(HALF_TILES // 2, HALF_TILES)
            for first, end, parts in SEGMENTS:
                with pe.Fori(first, end) as blk:
                    with pe.Fori(0, GROUPS) as group:
                        step0 = pe.snap(blk * ST + group * UNROLL)
                        for u in range(UNROLL):
                            par, h_in = u % 2, h_parts[(u + 1) % 2]
                            pe.wait_ge(s_h[0], step0 + u + 1)
                            recur(par, 0, every, low, h_in)
                            recur(par, 1, first_b, low, h_in)
                            pe.wait_ge(s_h[1], step0 + u + 1)
                            recur(par, 0, every, high, h_in).then_inc(s_rec[0], 1)
                            recur(par, 1, last_b, low, h_in)
                            recur(par, 1, every, high, h_in).then_inc(s_rec[1], 1)
                            if parts & PROJ:
                                if u == 0 and parts & XT:
                                    pe.wait_ge(s_xt, ((blk * GROUPS + group + FIRST_TILES) // TILES + 1) * CHUNK_BLOCKS)
                                if u == 0 and not parts & XT:
                                    pe.wait_ge(s_xt, BLOCKS)
                                tile = blk * GROUPS + group + FIRST_TILES
                                if u == 0:
                                    pe.wait_ge(s_proj, tile)
                                project(tile, u)
                    if parts & XT:
                        transpose_staged_x(blk + AHEAD)
                    if parts & OUT:
                        transpose_h(blk - 1)
            transpose_h(BLOCKS - 1)

        @block.scalar
        def _(act):
            def high_parts(half):
                tiles = half_columns(wx_hi, half)
                for g0, g1, by in ((0, 3, half_scale), (3, 4, scale)):
                    for k in range(K):
                        a = nc.scalar.activation(tiles[:, k, g0:g1, :], w_columns(half, g0, g1)(wx_raw)[:, k, :, :],
                                                 ACT.Copy, scale=by[:, WX:WX + 1])
                a.then_inc(s_wx_hi, 1)

            def x_high(blk, bank=p_xt):
                act.wait_ge(s_xt_psum, blk + 1)
                nc.scalar.activation(xt_hi[:, :, ds((blk % XT_RING) * P, P)],
                                     bank[:, :].rearrange("p (k c) -> p k c", k=K),
                                     ACT.Copy, scale=scale[:, X:X + 1]).then_inc(s_xt_hi, 1)

            def keep_projection(tile, bank=p_proj):
                act.wait_ge(s_proj_psum, tile + 1)
                to = proj[:, ds(((tile // TILES) % 2) * CT, CT), ds(tile % TILES, 1), :]
                nc.scalar.activation(to.rearrange("p (q t) n b -> p q t (n b)", t=ST),
                                     bank[:, :].rearrange("p (q b t) -> p q t b", b=N, t=ST),
                                     ACT.Identity, scale=proj_unit[:, 0:1],
                                     bias=b_scaled[:, ds(tile % TILES, 1)]).then_inc(s_proj, 1)

            def seed(step, par):
                for half in range(2):
                    a = nc.scalar.activation(
                        rec_parts(par, half),
                        proj[:, ds(step % RING, 1), half * HALF_TILES:(half + 1) * HALF_TILES, :].rearrange("p t n b -> p (t n) b")
                        .unsqueeze(2).broadcast_to([P, HALF_TILES, 2, N]),
                        ACT.Copy)
                return a

            act.wait_ge(s_scales, 1)
            for blk in range(XT_RING):
                x_high(blk, XT_BANKS[blk % 2])
            for half in range(2):
                high_parts(half)
            act.wait_ge(s_wx_split, 2)
            with act.Fori(0, TILES // 2) as pair:
                for i in range(2):
                    keep_projection(pair * 2 + i, PROJ_BANKS[i])
            act.wait_ge(s_wh_split, 1)
            keep_projection(TILES, PROJ_BANKS[0])
            x_high(XT_RING)
            act.wait_ge(s_bank_set, 1)
            act.wait_ge(s_h0_added, 1)
            seed(0, 0).then_inc(s_seeded, 1)

            unit_reg = act.alloc_register("unit")
            act.reg_load(unit_reg, unit[0:1, 0:1].bitcast(i32))

            def keep_h(step, u):
                return nc.scalar.activation(h_hist[:, ds(step % (HRING * ST), 1), :, :].rearrange("p t k b -> p (t k b)"),
                                            h_now[u][:, :, :].rearrange("p k b -> p (k b)"), ACT.Copy)

            for first, end, parts in SEGMENTS:
                with act.Fori(first, end) as blk:
                    with act.Fori(0, GROUPS) as group:
                        step0 = act.snap(blk * ST + group * UNROLL)
                        for u in range(UNROLL):
                            if u == UNROLL - 1 and parts & PROJ:
                                act.wait_ge(s_proj, ((step0 + UNROLL) // CT + 1) * TILES)
                            seed(step0 + u + 1, (u + 1) % 2)
                            for half in range(2):
                                turn = step0 * 2 + (2 * u + half + 1)
                                act.wait_ge(s_summed, turn)
                                nc.scalar.activation(gates[half][:, 0:GATES * HB], summed[half][:, :], ACT.Tanh,
                                                     scale=unit_reg).then_inc(s_gates, 1)
                                if half == 0:
                                    keep_h(step0 + u + HRING * ST - 1, (u - 1) % UNROLL)
                                act.wait_ge(s_cell, turn)
                                nc.scalar.activation(tanh_c[half][:, :], gates[half][:, GATES * HB:], ACT.Tanh,
                                                     scale=0.5).then_inc(s_tanh_c, 1)
                        if parts & PROJ:
                            keep_projection(blk * GROUPS + group + FIRST_TILES)
                    if parts & XT:
                        x_high(blk + AHEAD)
            act.wait_ge(s_h[1], T + 1)
            keep_h(T - 1, UNROLL - 1).then_inc(s_h_last, 1)

        @block.vector
        def _(dve):
            chained = [0]

            def chain(instruction):
                chained[0] += 1
                instruction.then_inc(s_dve, 1)
                dve.wait_ge(s_dve, chained[0])

            def low_parts(raw, hi, lo, which, half):
                cut = [half_columns(w, half) for w in (hi, lo)]
                for g0, g1, by in ((0, 3, half_scale), (3, 4, scale)):
                    for k in range(K):
                        i = nc.vector.scalar_tensor_tensor(cut[1][:, k, g0:g1, :], w_columns(half, g0, g1)(raw)[:, k, :, :],
                                                           by[:, which:which + 1], cut[0][:, k, g0:g1, :],
                                                           ALU.mult, ALU.subtract)
                return i

            def x_low(blk, bank=p_xt):
                dve.wait_ge(s_xt_hi, blk + 1)
                nc.vector.scalar_tensor_tensor(xt_lo[:, :, ds((blk % XT_RING) * P, P)],
                                               bank[:, :].rearrange("p (k c) -> p k c", k=K), scale[:, X:X + 1],
                                               xt_hi[:, :, ds((blk % XT_RING) * P, P)],
                                               ALU.mult, ALU.subtract).then_inc(s_xt, 1)

            def add_x(blk):
                dve.wait_ge(s_out_psum, blk + 1)
                nc.vector.scalar_tensor_tensor(out_rows[:, ds(blk % 2, 1), :].rearrange("p s d -> p (s d)"), p_out[:, :],
                                               2.0 ** -H_EXP, x_rows[:, ds(blk % XRING, 1), :].rearrange("p s d -> p (s d)"),
                                               ALU.mult, ALU.add).then_inc(s_out_rows, 1)

            nc.vector.memset(h_now[UNROLL - 1][:, :, :], 0.0)
            for half in range(2):
                nc.vector.memset(gates[half][:, GATES * HB:], 0.0)
            for half in range(2):
                nc.vector.memset(h_parts[1][:, half * SL:(half + 1) * SL, :, :], 0.0).then_inc(s_h[half], 1)

            def most_of(to, of, axis):
                return nc.vector.tensor_reduce(to, of, axis=axis, op=ALU.max, apply_absolute_value=True)

            for k in range(K):
                dve.wait_ge(s_wx_in[k], 16)
                most_of(most_parts[:, 2 + k:3 + k], wx_raw[:, k, :], AX.X)
            dve.wait_ge(s_small_t, 1)
            most_of(most[:, H0:H0 + 1], p_set[:, TILES:TILES + K * N], AX.X)
            dve.wait_ge(s_x_late, 16 * N)
            most_of(most_parts[:, 1:2], x_late, AX.XY)
            dve.wait_ge(s_x_in, 16 * N * 6)
            most_of(most_parts[:, 0:1], x_rows[:, :, :], AX.XY)
            for k in range(K):
                dve.wait_ge(s_wh_in[k], 16)
                i = most_of(most_parts[:, 2 + K + k:3 + K + k], wh_raw[:, k, :], AX.X)
            chain(i)
            for which, lo, hi in ((X, 0, 2), (WX, 2, 2 + K), (WH, 2 + K, 2 + 2 * K)):
                i = nc.vector.tensor_reduce(most[:, which:which + 1], most_parts[:, lo:hi], axis=AX.X, op=ALU.max)
            i.then_inc(s_most, 1)
            dve.wait_ge(s_most_t, 1)
            chain(nc.vector.tensor_reduce(top[:, :], p_out[0:4, 0:P], axis=AX.X, op=ALU.max))
            chain(nc.vector.tensor_scalar(top[:, :], top[:, :], LEAST, None, ALU.max))
            chain(nc.vector.tensor_scalar(top[:, :].bitcast(i32), top[:, :].bitcast(i32), (255 << 23), None, ALU.bitwise_and))
            nc.vector.tensor_scalar(top_diag[:, :], ident[0:4, 0:4], top[:, 0:1], None, ALU.mult).then_inc(s_top, 1)
            dve.wait_ge(s_power, 1)
            chain(nc.vector.tensor_copy(power[:, :], p_out[:, P:P + 4]))
            chain(nc.vector.tensor_scalar(scale[:, :].bitcast(i32), power[:, :].bitcast(i32), -1.0,
                                          float((2 * BIAS + TOP_EXP) * ONE_EXPONENT), ALU.mult, ALU.add))
            nc.vector.tensor_scalar(half_scale[:, :], scale[:, :], 0.5, None, ALU.mult)
            nc.vector.tensor_scalar(unit[:, :], power[:, WH:WH + 1], 2.0 ** -(TOP_EXP + H_EXP), None, ALU.mult)
            chain(nc.vector.tensor_scalar(bias_unit[:, :], scale[:, WH:WH + 1], 2.0 ** (H_EXP - 1), None, ALU.mult))
            nc.vector.tensor_scalar(bias_unit_half[:, :], bias_unit[:, :], 0.5, None, ALU.mult)
            nc.vector.tensor_scalar(h0_unit[:, :], power[:, H0:H0 + 1], 2.0 ** (H_EXP - 1 - TOP_EXP), None, ALU.mult)
            chain(nc.vector.tensor_scalar(proj_tmp[:, 0:1], bias_unit[:, :], 2.0 ** (-2 * TOP_EXP), None, ALU.mult))
            chain(nc.vector.tensor_tensor(proj_tmp[:, 1:2], proj_tmp[:, 0:1], power[:, X:X + 1], ALU.mult))
            chain(nc.vector.tensor_tensor(proj_unit[:, :], proj_tmp[:, 1:2], power[:, WX:WX + 1], ALU.mult))
            for half in range(2):
                b_t = p_set[:, 0:TILES].rearrange("p (g v s) -> p g v s", g=GATES, v=2)[:, :, half, :]
                to = b_scaled[:, half * HALF_TILES:(half + 1) * HALF_TILES].rearrange("p (g s) -> p g s", g=GATES)
                nc.vector.tensor_scalar(to[:, 0:3, :], b_t[:, 0:3, :], bias_unit_half[:, 0:1], None, ALU.mult)
                nc.vector.tensor_scalar(to[:, 3:4, :], b_t[:, 3:4, :], bias_unit[:, 0:1], None, ALU.mult)
            h0_t = p_set[:, TILES:TILES + K * N].rearrange("p (k b) -> p k b", k=K)
            chain(nc.vector.tensor_scalar(h0_parts[:, :, 0, :], h0_t, scale[:, H0:H0 + 1], None, ALU.mult))
            nc.vector.scalar_tensor_tensor(h0_parts[:, :, 1, :], h0_t, scale[:, H0:H0 + 1], h0_parts[:, :, 0, :],
                                           ALU.mult, ALU.subtract)
            nc.vector.tensor_copy(proj_tmp[:, 0:1], proj_tmp[:, 1:2]).then_inc(s_scales, 1)
            for blk in range(XT_RING):
                x_low(blk, XT_BANKS[blk % 2])
            for half in range(2):
                dve.wait_ge(s_wx_hi, half + 1)
                low_parts(wx_raw, wx_hi, wx_lo, WX, half).then_inc(s_wx_split, 1)
            dve.wait_ge(s_wh_hi, 1)
            low_parts(wh_raw, wh_hi, wh_lo, WH, 0)
            low_parts(wh_raw, wh_hi, wh_lo, WH, 1).then_inc(s_wh_split, 1)
            dve.wait_ge(s_h0_prod, 1)
            chain(nc.vector.tensor_reduce(h0_sum[:, :, :], p_set[:, 0:TILES * 2 * N].rearrange("p (n s b) -> p n b s", s=2, b=N),
                                          axis=AX.X, op=ALU.add))
            dve.wait_ge(s_proj, TILES)
            nc.vector.scalar_tensor_tensor(proj[:, 0, :, :], h0_sum[:, :, :], h0_unit[:, 0:1], proj[:, 0, :, :],
                                           ALU.mult, ALU.add).then_inc(s_h0_added, 1)
            x_low(XT_RING)

            def turn(half, u, step0):
                return step0 * 2 + (2 * u + half + 1)

            def sum_gates(half, u, step0):
                dve.wait_ge(s_rec[half], step0 + u + 1)
                nc.vector.tensor_reduce(summed[half][:, :].rearrange("p (n b) -> p n b", b=N),
                                        rec_parts(u % 2, half).rearrange("p n s b -> p n b s"),
                                        axis=AX.X, op=ALU.add).then_inc(s_summed, 1)

            def new_cell(half, u, step0):
                gate = gates[half]
                dve.wait_ge(s_gates, turn(half, u, step0))
                nc.vector.scalar_tensor_tensor(products[half][:, :], gate[:, 0:2 * HB], 1.0, gate[:, 3 * HB:5 * HB],
                                               ALU.add, ALU.mult).then_inc(s_products, 1)
                nc.vector.tensor_scalar(o_scaled[half][:, :], gate[:, 2 * HB:3 * HB], 1.0, 2.0 ** (H_EXP - 1),
                                        ALU.add, ALU.mult)
                dve.wait_ge(s_products, turn(half, u, step0))
                nc.vector.scalar_tensor_tensor(gate[:, 4 * HB:5 * HB], products[half][:, HB:2 * HB], 0.5,
                                               products[half][:, 0:HB], ALU.mult, ALU.add).then_inc(s_cell, 1)

            def new_h(half, u, step0):
                slices = slice(half * SL, (half + 1) * SL)
                whole = h_now[u][:, slices, :]
                high, low = h_parts[u % 2][:, slices, 0, :], h_parts[u % 2][:, slices, 1, :]
                o3 = o_scaled[half][:, :].rearrange("p (s b) -> p s b", s=SL)
                tanh3 = tanh_c[half][:, :].rearrange("p (s b) -> p s b", s=SL)
                dve.wait_ge(s_tanh_c, turn(half, u, step0))
                nc.vector.tensor_tensor(high, o3, tanh3, ALU.mult)
                nc.vector.tensor_tensor(whole, o3, tanh3, ALU.mult).then_inc(s_h_made, 1)
                dve.wait_ge(s_h_made, turn(half, u, step0))
                nc.vector.tensor_tensor(low, whole, high, ALU.subtract).then_inc(s_h[half], 1)

            for first, end, parts in SEGMENTS:
                with dve.Fori(first, end) as blk:
                    with dve.Fori(0, GROUPS) as group:
                        step0 = dve.snap(blk * ST + group * UNROLL)
                        for u in range(UNROLL):
                            sum_gates(0, u, step0)
                            new_cell(0, u, step0)
                            sum_gates(1, u, step0)
                            new_h(0, u, step0)
                            new_cell(1, u, step0)
                            new_h(1, u, step0)
                    if parts & XT:
                        x_low(blk + AHEAD)
                    if parts & OUT:
                        dve.wait_ge(s_stored, 16 * N * (blk - 1))
                        add_x(blk - 1)
            dve.wait_ge(s_stored, 16 * N * (BLOCKS - 1))
            add_x(BLOCKS - 1)


_INS = ["x", "cond_1024", "L0_cond_Wx", "L0_cond_Wh", "L0_cond_b"]
_OUTS = [((8, 512, 512), "float32")]


def kernel(**inputs):
    import numpy as _np
    import concourse.bacc as _bacc
    from concourse import mybir as _mybir
    from concourse.bass_utils import run_bass_kernel_spmd as _run

    nc = _bacc.Bacc("TRN2", target_bir_lowering=False, num_devices=1)
    arrays, args = {}, []
    for name in _INS:
        a = _np.ascontiguousarray(inputs[name])
        arrays[f"in_{name}_dram"] = a
        args.append(nc.dram_tensor(f"in_{name}_dram", a.shape, _mybir.dt.from_np(a.dtype), kind="ExternalInput").ap())
    for i, (shape, dtype) in enumerate(_OUTS):
        dt = _mybir.dt.from_np(_np.dtype(dtype))
        args.append(nc.dram_tensor(f"out_{i}_dram", shape, dt, kind="ExternalOutput").ap())
    lstm_residual_kernel(nc, *args)
    r = _run(nc, [arrays], core_ids=[0])
    got = tuple(r.results[0][f"out_{i}_dram"] for i in range(len(_OUTS)))
    return got[0]
```

```python
import concourse.bass as bass
from concourse import mybir
from contextlib import ExitStack


def lstm_residual_kernel(nc, x, h0, wx, wh, b, out):
    fp32, fp16, i32 = mybir.dt.float32, mybir.dt.float16, mybir.dt.int32
    ALU = mybir.AluOpType
    ACT = mybir.ActivationFunctionType
    AX = mybir.AxisListType
    ds = bass.ds

    P = 128
    N, T, D = x.shape
    H = wh.shape[0]
    K = H // P
    GATES = 4
    TILES = GATES * H // P
    CUTS = ((0, 1), (1, 3), (3, 4))
    CUT_TILE = (0, 4, 12)
    WIDTHS = tuple(e - f for f, e in CUTS)
    C = len(CUTS)
    ST = P // N
    BLOCKS = T // ST
    CHUNK_BLOCKS = 2
    CT = CHUNK_BLOCKS * ST
    CW = CT * N
    PAIRS = TILES // 2
    UNROLL = K
    GROUPS = ST // UNROLL
    RING = 2 * CT
    XRING = 16
    XT_RING = 2 * CHUNK_BLOCKS
    HRING = 2
    AHEAD = XT_RING
    PIECES = K
    FIRST_PAIRS = PAIRS + 1
    COLS = 2 * 2 * N
    assert K == 4 and GROUPS == PIECES and D == H and ST * N == P and 2 * CW == 512 and XRING * 2 == BLOCKS

    H_EXP, TOP_EXP, LEAST = 14, 14, 2.0 ** -60
    ONE_EXPONENT = 1 << 23
    BIAS = 127
    WH, WX, X, H0 = range(4)

    def cut_tiles(cut):
        return range(CUT_TILE[cut], CUT_TILE[cut] + GATES * WIDTHS[cut])

    def cut_raw(w, cut):
        return w.rearrange("p k (g c) -> p k g c", g=GATES)[:, :, :, CUTS[cut][0] * P:CUTS[cut][1] * P]

    def cut_columns(w, cut):
        tiles = cut_tiles(cut)
        return w[:, :, tiles[0] * P:(tiles[-1] + 1) * P].rearrange("p k (g c) -> p k g c", g=GATES)

    ctx = ExitStack()
    with ctx:
        def sb(name, shape, dt):
            return ctx.enter_context(nc.sbuf_tensor(name, shape, dt))

        def pb(name, shape, dt):
            return ctx.enter_context(nc.psum_tensor(name, shape, dt))

        def sem(name):
            return ctx.enter_context(nc.semaphore(name))

        wh_parts = sb("wh_parts", [P, 2, K, TILES * P], fp16)
        wh_hi, wh_lo = wh_parts[:, 0, :, :], wh_parts[:, 1, :, :]
        x_late = wh_parts[:, :, :, :].rearrange("p s k n -> p (s k n)").bitcast(fp32).rearrange("p (s d) -> p s d", d=D)
        wx_hi = sb("wx_hi", [P, K, TILES * P], fp16)
        wx_lo = sb("wx_lo", [P, K, TILES * P], fp16)
        proj = sb("proj", [P, 2 * RING, TILES, N], fp32)
        flat_proj = proj[:, :, :, :].rearrange("p t n b -> p (t n b)")
        wx_raw = flat_proj[:, 0:K * TILES * P].rearrange("p (k n) -> p k n", k=K)
        wh_raw = flat_proj[:, K * TILES * P:2 * K * TILES * P].rearrange("p (k n) -> p k n", k=K)
        x_rows = sb("x_rows", [P, XRING, D], fp32)
        x_scaled = sb("x_scaled", [P, D], fp32)
        x_parts = sb("x_parts", [P, 2, D], fp16)
        xt_hi = sb("xt_hi", [P, K, XT_RING * P], fp16)
        xt_lo = sb("xt_lo", [P, K, XT_RING * P], fp16)
        h_hist = sb("h_hist", [P, HRING * K, 2, N, ST], fp16)
        h_now = [sb(f"h_now{i}", [P, K, N], fp32) for i in range(2)]
        out_rows = sb("out_rows", [P, 2, D], fp32)
        h_parts = [sb(f"h_parts{i}", [P, K, 2, N], fp16) for i in range(2)]
        GC = [width * N for width in WIDTHS]
        gates = [sb(f"gates{v}", [P, (GATES + 2) * GC[v]], fp32) for v in range(C)]
        summed = [sb(f"summed{v}", [P, GATES * GC[v]], fp32) for v in range(C)]
        products = [sb(f"products{v}", [P, 3 * GC[v]], fp32) for v in range(C)]
        tanh_c = [sb(f"tanh_c{v}", [P, GC[v]], fp32) for v in range(C)]
        ident = sb("ident", [P, P], fp32)
        ident16 = sb("ident16", [P, P], fp16)
        ones = sb("ones", [P, P], fp32)
        b_rows = sb("b_rows", [TILES, P], fp32)
        b_scaled = sb("b_scaled", [P, TILES], fp32)
        h0_rows = sb("h0_rows", [N, H], fp32)
        h0_parts = sb("h0_parts", [P, K, 2, N], fp16)
        h0_sum = sb("h0_sum", [P, TILES, N], fp32)
        most = sb("most", [P, 4], fp32)
        most_parts = sb("most_parts", [P, 2 + 2 * K], fp32)
        top = sb("top", [4, 1], fp32)
        top_diag = sb("top_diag", [4, 4], fp32)
        power = sb("power", [P, 4], fp32)
        scale = sb("scale", [P, 4], fp32)
        half_scale = sb("half_scale", [P, 4], fp32)
        unit = sb("unit", [P, 1], fp32)
        bias_unit = sb("bias_unit", [P, 1], fp32)
        bias_unit_half = sb("bias_unit_half", [P, 1], fp32)
        proj_tmp = sb("proj_tmp", [P, 3], fp32)
        proj_unit = sb("proj_unit", [P, 1], fp32)
        h0_unit = sb("h0_unit", [P, 1], fp32)

        rec = [pb(f"rec{v}", [P, 512], fp32) for v in range(C)]
        p_proj = pb("p_proj", [P, 2 * CW], fp32)
        p_xt = pb("p_xt", [P, K * P], fp32)
        p_xt_low = pb("p_xt_low", [P, P], fp32)
        p_out = pb("p_out", [P, K * P], fp32)
        p_set = pb("p_set", [P, 512], fp32)

        def rec_parts(cut):
            return rec[cut][:, 0:GATES * WIDTHS[cut] * COLS].rearrange("p (n s b) -> p n s b", s=COLS // N, b=N)[:, :, 0:2, :]

        XT_BANKS = [bank[:, 0:K * P] for bank in (p_xt, *rec)]
        PROJ_BANKS = (p_proj, p_out)

        def halves(bank):
            return [bank[:, 0:CW], bank[:, CW:2 * CW]]

        PAIR_BANKS = [p_proj[:, 0:CW], p_set[:, 0:CW]]

        s_wx_in = [sem(f"wx_in{k}") for k in range(K)]
        s_wh_in = [sem(f"wh_in{k}") for k in range(K)]
        s_small_in = sem("small_in")
        s_x_late = sem("x_late")
        s_x_in = sem("x_in")
        s_consts = sem("consts")
        s_small_t = sem("small_t")
        s_most = sem("most_done")
        s_dve = sem("dve_setup")
        s_most_t = sem("most_t")
        s_top = sem("top_ready")
        s_power = sem("power_psum")
        s_scales = sem("scales_ready")
        s_wx_hi = sem("wx_hi_ready")
        s_wh_hi = sem("wh_hi_ready")
        s_wx_split = sem("wx_split")
        s_wh_split = sem("wh_split")
        s_h0_prod = sem("h0_prod")
        s_h0_added = sem("h0_added")
        s_bank_set = sem("bank_bits_set")
        s_x_scaled = sem("x_scaled")
        s_x_high = sem("x_high_part")
        s_x_parts = sem("x_parts_ready")
        s_xt_psum = sem("xt_psum")
        s_xt_hi = sem("xt_hi_ready")
        s_xt = sem("xt_lo_ready")
        s_proj_psum = sem("proj_psum")
        s_proj = sem("proj_ready")
        s_seeded = sem("seeded")
        s_rec = [sem(f"rec{v}") for v in range(C)]
        s_h = [sem(f"h{v}") for v in range(C)]
        s_summed = sem("summed_ready")
        s_gates = sem("gates_ready")
        s_products = sem("products_ready")
        s_cell = sem("cell_ready")
        s_tanh_c = sem("tanh_c_ready")
        s_h_made = sem("h_made")
        s_h_kept = sem("h_kept")
        s_out_psum = sem("out_psum")
        s_out_rows = sem("out_rows_ready")
        s_stored = sem("stored")

        PROJ, XT, OUT = 1, 2, 4
        xt_end = BLOCKS - AHEAD
        proj_end = BLOCKS - CHUNK_BLOCKS
        SEGMENTS = [(0, 1, PROJ | XT), (1, xt_end, PROJ | XT | OUT),
                    (xt_end, proj_end, PROJ | OUT), (proj_end, BLOCKS, OUT)]

        block = ctx.enter_context(nc.Block())

        @block.sync
        def _(sp):
            for k in range(K):
                sp.dma_start(wx_raw[:, k, :], wx[k * P:(k + 1) * P, :]).then_inc(s_wx_in[k], 16)
            sp.dma_start(b_rows[:, :], b.rearrange("(n c) -> n c", c=P)).then_inc(s_small_in, 16)
            sp.dma_start(h0_rows[:, :], h0).then_inc(s_small_in, 16)
            for n in range(N):
                sp.dma_start(x_late[n * ST:(n + 1) * ST, :, :],
                             x[n, XRING * ST:, :].rearrange("(s t) d -> t s d", t=ST)).then_inc(s_x_late, 16)
            for n in range(N):
                sp.dma_start(x_rows[n * ST:(n + 1) * ST, :, :],
                             x[n, 0:XRING * ST, :].rearrange("(s t) d -> t s d", t=ST)).then_inc(s_x_in, 16 * 6)
            for k in range(K):
                sp.dma_start(wh_raw[:, k, :], wh[k * P:(k + 1) * P, :]).then_inc(s_wh_in[k], 16)

            def store(blk):
                sp.wait_ge(s_out_rows, (blk + 1) * PIECES + 1)
                for n in range(N):
                    sp.dma_start(out[n, ds(blk * ST, ST), :],
                                 out_rows[n * ST:(n + 1) * ST, ds(blk % 2, 1), :].rearrange("p s d -> p (s d)")
                                 ).then_inc(s_stored, 16)

            with sp.Fori(0, XRING) as blk:
                store(blk)
                for n in range(N):
                    sp.dma_start(x_rows[n * ST:(n + 1) * ST, ds(blk % XRING, 1), :].rearrange("p s d -> p (s d)"),
                                 x[n, ds((blk + XRING) * ST, ST), :]).then_inc(s_x_in, 16)
            with sp.Fori(XRING, BLOCKS) as blk:
                store(blk)
            sp.wait_ge(s_stored, 16 * N * (BLOCKS + 1))

        @block.gpsimd
        def _(pool):
            nc.gpsimd.memset(ident[:, :], 0.0).then_inc(s_consts, 1)
            pool.wait_ge(s_consts, 1)
            nc.gpsimd.affine_select(out=ident[:, :], in_=ident[:, :], compare_op=ALU.not_equal, fill=1.0,
                                    base=0, pattern=[[-1, P]], channel_multiplier=1).then_inc(s_consts, 1)
            nc.gpsimd.memset(ones[:, :], 1.0).then_inc(s_consts, 1)
            pool.wait_ge(s_consts, 3)
            nc.gpsimd.tensor_copy(ident16[:, :], ident[:, :]).then_inc(s_consts, 1)

            def split_x(blk):
                nc.gpsimd.tensor_tensor(x_scaled[:, :], x_rows[:, ds(blk % XRING, 1), :].rearrange("p s d -> p (s d)"),
                                        scale[:, X:X + 1].broadcast_to([P, D]), ALU.mult).then_inc(s_x_scaled, 1)
                pool.wait_ge(s_xt_psum, blk * PIECES)
                pool.wait_ge(s_x_scaled, blk - XT_RING + 1)
                nc.gpsimd.tensor_tensor(x_parts[:, 0, :], x_scaled[:, :], ones[:, 0:1].broadcast_to([P, D]), ALU.mult).then_inc(s_x_high, 1)
                pool.wait_ge(s_x_high, blk - XT_RING + 1)
                nc.gpsimd.tensor_tensor(x_parts[:, 1, :], x_scaled[:, :], x_parts[:, 0, :], ALU.subtract
                                        ).then_inc(s_x_parts, PIECES)
                pool.wait_ge(s_x_parts, (blk - XT_RING + 1) * PIECES)

            pool.wait_ge(s_scales, 1)
            for cut in (0, 2):
                for g0, g1, by in ((0, 3, half_scale), (3, 4, scale)):
                    i = nc.gpsimd.tensor_scalar(cut_columns(wh_hi, cut)[:, :, g0:g1, :], cut_raw(wh_raw, cut)[:, :, g0:g1, :],
                                                by[:, WH:WH + 1], None, ALU.mult)
            i.then_inc(s_wh_hi, 1)
            with pool.Fori(XT_RING, XRING) as blk:
                split_x(blk)
            with pool.Fori(XRING, BLOCKS) as blk:
                pool.wait_ge(s_x_in, 16 * N * (blk - XRING + 7))
                split_x(blk)

        @block.tensor
        def _(pe):
            def transpose_x(bank, rows):
                for k in range(K):
                    t = nc.tensor.transpose(bank[:, k * P:(k + 1) * P], rows[:, k * P:(k + 1) * P], ident[:, :])
                t.then_inc(s_xt_psum, PIECES)

            def transpose_x_piece(at):
                for part, bank in enumerate((p_xt, p_xt_low)):
                    t = nc.tensor.matmul(bank[:, 0:P], x_parts[:, part, ds(at, P)], ident16[:, :], start=True, stop=True)
                t.then_inc(s_xt_psum, 1)

            def transpose_h(piece, to):
                for part in range(2):
                    rows = h_hist[:, ds(piece, 1), part, :, :].rearrange("p k b t -> p (k b t)")
                    t = nc.tensor.matmul(to, rows, ident16[:, :], start=(part == 0), stop=(part == 1))
                return t

            def project(w_at, x_at, k, banks, tiles=range(2), beside=None):
                for i, (w, xt) in enumerate(((wx_hi, xt_hi), (wx_hi, xt_lo), (wx_lo, xt_hi))):
                    for tile in tiles:
                        m = nc.tensor.matmul(banks[tile], w[:, k, ds(w_at + tile * P, P)], xt[:, k, ds(x_at, CW)],
                                             start=(k == 0 and i == 0), stop=(k == K - 1 and i == 2))
                    if i == 1 and beside:
                        beside()
                if k == K - 1 and tiles[-1] == 1:
                    m.then_inc(s_proj_psum, 1)

            def recur(cut, of, parts, first=0, end=None):
                for i, n in list(enumerate(cut_tiles(cut)))[first:end]:
                    for k in range(*CUTS[of]):
                        for w in (wh_hi, wh_lo):
                            m = nc.tensor.matmul(rec[cut][:, i * COLS:(i + 1) * COLS], w[:, k, n * P:(n + 1) * P],
                                                 parts[:, k, :, :].rearrange("p s b -> p (s b)")
                                                 .unsqueeze(1).broadcast_to([P, COLS // (2 * N), 2 * N]),
                                                 start=False, stop=True, skip_group_check=True)
                return m

            pe.wait_ge(s_consts, 4)
            pe.wait_ge(s_small_in, 32)
            nc.tensor.transpose(p_set[:, 0:TILES], b_rows[:, :], ident[0:TILES, 0:TILES])
            for k in range(K):
                t = nc.tensor.transpose(p_set[:, TILES + k * N:TILES + (k + 1) * N],
                                        h0_rows[:, k * P:(k + 1) * P], ident[0:N, 0:N])
            t.then_inc(s_small_t, 1)
            pe.wait_ge(s_x_in, 16 * N * 6)
            for blk in range(XT_RING):
                transpose_x(XT_BANKS[blk], x_rows[:, blk, :])
            pe.wait_ge(s_most, 1)
            nc.tensor.transpose(p_out[0:4, 0:P], most[:, :], ident[:, :]).then_inc(s_most_t, 1)
            pe.wait_ge(s_top, 1)
            nc.tensor.matmul(p_out[:, P:P + 4], ones[0:4, :], top_diag[:, :], start=True, stop=True).then_inc(s_power, 1)

            def project_pair(pair, i):
                for tile in range(2):
                    for k in range(K):
                        project((pair % PAIRS) * 2 * P, ((pair // PAIRS) % 2) * CW, k, halves(PROJ_BANKS[i]), [tile])

            pe.wait_ge(s_xt, XT_RING * PIECES)
            for bank in rec:
                for n in range(2):
                    m = nc.tensor.matmul(bank[:, n * P:(n + 1) * P], ident[:, :], ident[:, :],
                                         start=(n == 0), stop=True, skip_group_check=True)
            m.then_inc(s_bank_set, 1)
            pe.wait_ge(s_wx_split, 1)
            for i in range(2):
                project_pair(i, i)
            for cut, (first, end) in ((1, (1, 3)), (2, (3, 4))):
                pe.wait_ge(s_wx_split, cut + 1)
                with pe.Fori(first, end) as two:
                    for i in range(2):
                        pe.wait_ge(s_proj, two * 2 + i - 1)
                        project_pair(two * 2 + i, i)
            pe.wait_ge(s_wh_split, 1)
            for n in range(TILES):
                for k in range(K):
                    for i, w in enumerate((wh_hi, wh_lo)):
                        m = nc.tensor.matmul(p_set[:, n * 2 * N:(n + 1) * 2 * N], w[:, k, n * P:(n + 1) * P],
                                             h0_parts[:, k, :, :].rearrange("p s b -> p (s b)"),
                                             start=(k == 0 and i == 0), stop=(k == K - 1 and i == 1))
            m.then_inc(s_h0_prod, 1)
            pe.wait_ge(s_proj, PAIRS - 1)
            project_pair(PAIRS, 0)
            pe.wait_ge(s_seeded, 1)

            w_reg, x_reg = pe.alloc_register("w_at"), pe.alloc_register("x_at")

            def place_w(pair):
                pe.reg_mov(w_reg, (pair % PAIRS) * 2 * P)

            def place_x(pair):
                pe.reg_mov(x_reg, ((pair // PAIRS) % 2) * CW)

            place_w(FIRST_PAIRS)
            place_x(FIRST_PAIRS)
            for first, end, parts in SEGMENTS:
                with pe.Fori(first * GROUPS, end * GROUPS) as turn:
                    step0 = pe.snap(turn * UNROLL)
                    if parts & PROJ:
                        pair = pe.snap(turn + FIRST_PAIRS)
                        w_at = pe.snap(w_reg, min_val=0, max_val=(PAIRS - 1) * 2 * P)
                        x_at = pe.snap(x_reg, min_val=0, max_val=CW)
                    for u in range(UNROLL):
                        h_in = h_parts[(u + 1) % 2]
                        steps = pe.snap(step0 + (u + 1))
                        pe.wait_ge(s_h[0], steps)
                        recur(0, 0, h_in)
                        pe.wait_ge(s_seeded, steps)
                        recur(1, 0, h_in)
                        pe.wait_ge(s_h[1], steps)
                        recur(0, 1, h_in)
                        recur(1, 1, h_in, 0, K)
                        pe.wait_ge(s_h[2], steps)
                        recur(0, 2, h_in).then_inc(s_rec[0], 1)
                        recur(1, 1, h_in, K, 2 * K)
                        recur(1, 2, h_in).then_inc(s_rec[1], 1)
                        for of in range(C):
                            m = recur(2, of, h_in)
                        m.then_inc(s_rec[2], 1)
                        if u == 2 and parts & XT:
                            pe.wait_ge(s_xt_hi, turn + (AHEAD * PIECES + 1))
                            pe.wait_ge(s_xt, turn + (AHEAD * PIECES + 1))
                        if u == 0 and parts & PROJ and not parts & XT:
                            pe.wait_ge(s_xt_hi, BLOCKS * PIECES)
                            pe.wait_ge(s_xt, BLOCKS * PIECES)
                        if parts & PROJ:
                            if u == 0:
                                pe.wait_ge(s_proj, pair)
                            project(w_at, x_at, u, PAIR_BANKS, range(2),
                                            {1: lambda: place_x(pair + 1), 2: lambda: place_w(pair + 1)}.get(u))
                        if u == 0 and parts & XT:
                            pe.wait_ge(s_x_parts, turn + 1)
                            transpose_x_piece((turn % PIECES) * P)
                        if u == 1 and parts & OUT:
                            pe.wait_ge(s_h_kept, step0)
                            pe.wait_ge(s_out_rows, turn - (PIECES - 1))
                            transpose_h((turn - PIECES) % (HRING * PIECES), p_out[:, 0:P]).then_inc(s_out_psum, 1)
            pe.wait_ge(s_h_kept, T)
            pe.wait_ge(s_out_rows, (BLOCKS - 1) * PIECES + 1)
            for k in range(PIECES):
                t = transpose_h((BLOCKS - 1) % HRING * PIECES + k, p_out[:, k * P:(k + 1) * P])
            t.then_inc(s_out_psum, 1)

        @block.scalar
        def _(act):
            def high_parts(raw, high, which, cut):
                for g0, g1, by in ((0, 3, half_scale), (3, 4, scale)):
                    a = nc.scalar.activation(cut_columns(high, cut)[:, :, g0:g1, :], cut_raw(raw, cut)[:, :, g0:g1, :],
                                             ACT.Copy, scale=by[:, which:which + 1])
                return a

            def x_high(blk, bank=p_xt):
                act.wait_ge(s_xt_psum, (blk + 1) * PIECES)
                nc.scalar.activation(xt_hi[:, :, ds((blk % XT_RING) * P, P)],
                                     bank[:, :].rearrange("p (k c) -> p k c", k=K),
                                     ACT.Copy, scale=scale[:, X:X + 1]).then_inc(s_xt_hi, PIECES)

            def keep_projection(pair, banks, to=None):
                act.wait_ge(s_proj_psum, pair + 1)
                step, n = to or (((pair // PAIRS) % 2) * CT, (pair % PAIRS) * 2)
                for i in range(2):
                    a = nc.scalar.activation(
                        proj[:, ds(step, CT), ds(n + i, 1), :].rearrange("p (q t) n b -> p q t (n b)", t=ST),
                        banks[i].rearrange("p (q b t) -> p q t b", b=N, t=ST),
                        ACT.Identity, scale=proj_unit[:, 0:1], bias=b_scaled[:, ds(n + i, 1)])
                a.then_inc(s_proj, 1)

            def seed(cut, step):
                tiles = cut_tiles(cut)
                return nc.scalar.activation(
                    rec_parts(cut), proj[:, ds(step % RING, 1), tiles[0]:tiles[-1] + 1, :].rearrange("p t n b -> p (t n) b")
                    .unsqueeze(2).broadcast_to([P, len(tiles), 2, N]), ACT.Copy)

            act.wait_ge(s_consts, 4)
            nc.scalar.activation(proj_tmp[:, 2:3], ident[:, 0:1], ACT.Tanh)
            act.wait_ge(s_scales, 1)
            high_parts(wx_raw, wx_hi, WX, 0).then_inc(s_wx_hi, 1)
            for blk in range(XT_RING):
                x_high(blk, XT_BANKS[blk])
            for cut in (1, 2):
                high_parts(wx_raw, wx_hi, WX, cut).then_inc(s_wx_hi, 1)
            high_parts(wh_raw, wh_hi, WH, 1).then_inc(s_wh_hi, 1)
            act.wait_ge(s_wx_split, C)
            with act.Fori(0, PAIRS // 2) as two:
                for i in range(2):
                    keep_projection(two * 2 + i, halves(PROJ_BANKS[i]))
            keep_projection(PAIRS, halves(PROJ_BANKS[0]))
            act.wait_ge(s_bank_set, 1)
            act.wait_ge(s_h0_added, 1)
            seed(0, 0)
            seed(2, 0)
            seed(1, 0).then_inc(s_seeded, 1)

            unit_reg = act.alloc_register("unit")
            act.reg_load(unit_reg, unit[0:1, 0:1].bitcast(i32))

            def tanh_gates(cut, turn):
                act.wait_ge(s_summed, turn)
                nc.scalar.activation(gates[cut][:, 0:GATES * GC[cut]], summed[cut][:, :], ACT.Tanh,
                                     scale=unit_reg).then_inc(s_gates, 1)

            def tanh_cell(cut, turn):
                act.wait_ge(s_cell, turn)
                nc.scalar.activation(tanh_c[cut][:, :], gates[cut][:, GATES * GC[cut]:(GATES + 1) * GC[cut]], ACT.Tanh,
                                     scale=0.5).then_inc(s_tanh_c, 1)

            def keep_h(step, u):
                act.wait_ge(s_h[C - 1], step + 2)
                at = (step // ST) % HRING
                nc.scalar.activation(h_hist[:, ds(at * K, K), :, :, ds(step % ST, 1)].rearrange("p k s b t -> p (k s b t)"),
                                     h_parts[u % 2][:, :, :, :].rearrange("p k s b -> p (k s b)"), ACT.Copy).then_inc(s_h_kept, 1)

            def keep_x_piece(turn, at):
                act.wait_ge(s_xt_psum, turn + 1)
                nc.scalar.activation(xt_hi[:, :, :].rearrange("p k c -> p (k c)")[:, ds(at, P)],
                                     p_xt[:, 0:P], ACT.Copy).then_inc(s_xt_hi, 1)

            for first, end, parts in SEGMENTS:
                with act.Fori(first * GROUPS, end * GROUPS) as group_turn:
                    step0 = act.snap(group_turn * UNROLL)
                    blk, group = group_turn // PIECES, group_turn % PIECES
                    x_at = act.snap(group * (XT_RING * P) + (blk % XT_RING) * P)
                    pair = act.snap(group_turn + FIRST_PAIRS)
                    pair_at = (act.snap(((pair // PAIRS) % 2) * CT), act.snap((pair % PAIRS) * 2))
                    for u in range(UNROLL):
                        step = step0 + u
                        turns = [step * C + cut + 1 for cut in range(C)]
                        tanh_gates(0, turns[0])
                        if u == UNROLL - 1 and parts & PROJ:
                            act.wait_ge(s_proj, pair)
                        seed(0, step + 1)
                        tanh_cell(0, turns[0])
                        tanh_gates(1, turns[1])
                        seed(1, step + 1).then_inc(s_seeded, 1)
                        tanh_cell(1, turns[1])
                        tanh_gates(2, turns[2])
                        seed(2, step + 1)
                        tanh_cell(2, turns[2])
                        if u == 0 and parts & XT:
                            keep_x_piece(group_turn + AHEAD * PIECES, x_at)
                        if u == UNROLL - 1 and parts & PROJ:
                            keep_projection(pair, PAIR_BANKS, pair_at)
                        keep_h(step, u)

        @block.vector
        def _(dve):
            chained = [0]

            def chain(instruction):
                chained[0] += 1
                instruction.then_inc(s_dve, 1)
                dve.wait_ge(s_dve, chained[0])

            def low_parts(raw, hi, lo, which, cut):
                for g in range(GATES):
                    by = scale if g == GATES - 1 else half_scale
                    i = nc.vector.scalar_tensor_tensor(cut_columns(lo, cut)[:, :, g, :], cut_raw(raw, cut)[:, :, g, :],
                                                       by[:, which:which + 1], cut_columns(hi, cut)[:, :, g, :],
                                                       ALU.mult, ALU.subtract)
                return i

            def x_low(blk, bank=p_xt):
                dve.wait_ge(s_xt_hi, (blk + 1) * PIECES)
                nc.vector.scalar_tensor_tensor(xt_lo[:, :, ds((blk % XT_RING) * P, P)],
                                               bank[:, :].rearrange("p (k c) -> p k c", k=K), scale[:, X:X + 1],
                                               xt_hi[:, :, ds((blk % XT_RING) * P, P)],
                                               ALU.mult, ALU.subtract).then_inc(s_xt, PIECES)

            def keep_x_piece(turn, at):
                dve.wait_ge(s_xt_psum, turn + 1)
                nc.vector.tensor_copy(xt_lo[:, :, :].rearrange("p k c -> p (k c)")[:, ds(at, P)],
                                      p_xt_low[:, :]).then_inc(s_xt, 1)

            def add_x(out_at, x_at, h):
                width = h.shape[1]
                return nc.vector.scalar_tensor_tensor(out_rows[:, :, :].rearrange("p s d -> p (s d)")[:, ds(out_at, width)], h,
                                                      2.0 ** -H_EXP,
                                                      x_rows[:, :, :].rearrange("p s d -> p (s d)")[:, ds(x_at, width)],
                                                      ALU.mult, ALU.add).then_inc(s_out_rows, width // P)

            for cut in range(C):
                nc.vector.memset(gates[cut][:, (GATES + 1) * GC[cut]:], 2.0 ** (H_EXP - 1))
                i = nc.vector.memset(gates[cut][:, GATES * GC[cut]:(GATES + 1) * GC[cut]], 0.0)
                if cut < 2:
                    i.then_inc(*((s_stored, 16 * N), (s_out_rows, 1))[cut])
            for cut in range(C):
                nc.vector.memset(h_parts[1][:, CUTS[cut][0]:CUTS[cut][1], :, :], 0.0).then_inc(s_h[cut], 1)

            def most_of(to, of, axis):
                return nc.vector.tensor_reduce(to, of, axis=axis, op=ALU.max, apply_absolute_value=True)

            for k in range(K):
                dve.wait_ge(s_wx_in[k], 16)
                most_of(most_parts[:, 2 + k:3 + k], wx_raw[:, k, :], AX.X)
            dve.wait_ge(s_small_t, 1)
            most_of(most[:, H0:H0 + 1], p_set[:, TILES:TILES + K * N], AX.X)
            dve.wait_ge(s_x_late, 16 * N)
            most_of(most_parts[:, 1:2], x_late, AX.XY)
            dve.wait_ge(s_x_in, 16 * N * 6)
            most_of(most_parts[:, 0:1], x_rows[:, :, :], AX.XY)
            for k in range(K):
                dve.wait_ge(s_wh_in[k], 16)
                i = most_of(most_parts[:, 2 + K + k:3 + K + k], wh_raw[:, k, :], AX.X)
            chain(i)
            for which, lo, hi in ((X, 0, 2), (WX, 2, 2 + K), (WH, 2 + K, 2 + 2 * K)):
                i = nc.vector.tensor_reduce(most[:, which:which + 1], most_parts[:, lo:hi], axis=AX.X, op=ALU.max)
            i.then_inc(s_most, 1)
            dve.wait_ge(s_most_t, 1)
            chain(nc.vector.tensor_reduce(top[:, :], p_out[0:4, 0:P], axis=AX.X, op=ALU.max))
            chain(nc.vector.tensor_scalar(top[:, :], top[:, :], LEAST, None, ALU.max))
            chain(nc.vector.tensor_scalar(top[:, :].bitcast(i32), top[:, :].bitcast(i32), (255 << 23), None, ALU.bitwise_and))
            nc.vector.tensor_scalar(top_diag[:, :], ident[0:4, 0:4], top[:, 0:1], None, ALU.mult).then_inc(s_top, 1)
            dve.wait_ge(s_power, 1)
            chain(nc.vector.tensor_copy(power[:, :], p_out[:, P:P + 4]))
            chain(nc.vector.tensor_scalar(scale[:, :].bitcast(i32), power[:, :].bitcast(i32), -1.0,
                                          float((2 * BIAS + TOP_EXP) * ONE_EXPONENT), ALU.mult, ALU.add))
            nc.vector.tensor_scalar(half_scale[:, :], scale[:, :], 0.5, None, ALU.mult)
            nc.vector.tensor_scalar(unit[:, :], power[:, WH:WH + 1], 2.0 ** -(TOP_EXP + H_EXP), None, ALU.mult)
            chain(nc.vector.tensor_scalar(bias_unit[:, :], scale[:, WH:WH + 1], 2.0 ** (H_EXP - 1), None, ALU.mult))
            nc.vector.tensor_scalar(bias_unit_half[:, :], bias_unit[:, :], 0.5, None, ALU.mult)
            nc.vector.tensor_scalar(h0_unit[:, :], power[:, H0:H0 + 1], 2.0 ** (H_EXP - 1 - TOP_EXP), None, ALU.mult)
            chain(nc.vector.tensor_scalar(proj_tmp[:, 0:1], bias_unit[:, :], 2.0 ** (-2 * TOP_EXP), None, ALU.mult))
            chain(nc.vector.tensor_tensor(proj_tmp[:, 1:2], proj_tmp[:, 0:1], power[:, X:X + 1], ALU.mult))
            chain(nc.vector.tensor_tensor(proj_unit[:, :], proj_tmp[:, 1:2], power[:, WX:WX + 1], ALU.mult))
            for cut, (first, end) in enumerate(CUTS):
                b_t = p_set[:, 0:TILES].rearrange("p (g s) -> p g s", g=GATES)[:, :, first:end]
                tiles = cut_tiles(cut)
                to = b_scaled[:, tiles[0]:tiles[-1] + 1].rearrange("p (g s) -> p g s", g=GATES)
                nc.vector.tensor_scalar(to[:, 0:3, :], b_t[:, 0:3, :], bias_unit_half[:, 0:1], None, ALU.mult)
                nc.vector.tensor_scalar(to[:, 3:4, :], b_t[:, 3:4, :], bias_unit[:, 0:1], None, ALU.mult)
            h0_t = p_set[:, TILES:TILES + K * N].rearrange("p (k b) -> p k b", k=K)
            chain(nc.vector.tensor_scalar(h0_parts[:, :, 0, :], h0_t, scale[:, H0:H0 + 1], None, ALU.mult))
            nc.vector.scalar_tensor_tensor(h0_parts[:, :, 1, :], h0_t, scale[:, H0:H0 + 1], h0_parts[:, :, 0, :],
                                           ALU.mult, ALU.subtract)
            nc.vector.tensor_copy(proj_tmp[:, 0:1], proj_tmp[:, 1:2]).then_inc(s_scales, 1)
            for cut in range(C):
                dve.wait_ge(s_wx_hi, cut + 1)
                low_parts(wx_raw, wx_hi, wx_lo, WX, cut).then_inc(s_wx_split, 1)
                if cut == 0:
                    for blk in range(XT_RING):
                        x_low(blk, XT_BANKS[blk])
            dve.wait_ge(s_wh_hi, 2)
            for cut in range(C):
                i = low_parts(wh_raw, wh_hi, wh_lo, WH, cut)
            i.then_inc(s_wh_split, 1)
            dve.wait_ge(s_h0_prod, 1)
            chain(nc.vector.tensor_reduce(h0_sum[:, :, :], p_set[:, 0:TILES * 2 * N].rearrange("p (n s b) -> p n b s", s=2, b=N),
                                          axis=AX.X, op=ALU.add))
            dve.wait_ge(s_proj, PAIRS)
            nc.vector.scalar_tensor_tensor(proj[:, 0, :, :], h0_sum[:, :, :], h0_unit[:, 0:1], proj[:, 0, :, :],
                                           ALU.mult, ALU.add).then_inc(s_h0_added, 1)

            def sum_gates(cut, step):
                dve.wait_ge(s_rec[cut], step + 1)
                nc.vector.tensor_reduce(summed[cut][:, :].rearrange("p (n b) -> p n b", b=N),
                                        rec_parts(cut).rearrange("p n s b -> p n b s"),
                                        axis=AX.X, op=ALU.add).then_inc(s_summed, 1)

            def cell_products(cut, turn):
                gate, c = gates[cut], GC[cut]
                dve.wait_ge(s_gates, turn)
                nc.vector.scalar_tensor_tensor(products[cut][:, :], gate[:, 0:3 * c], 1.0, gate[:, 3 * c:6 * c],
                                               ALU.add, ALU.mult).then_inc(s_products, 1)

            def new_cell(cut, turn):
                c = GC[cut]
                dve.wait_ge(s_products, turn)
                nc.vector.scalar_tensor_tensor(gates[cut][:, 4 * c:5 * c], products[cut][:, c:2 * c], 0.5,
                                               products[cut][:, 0:c], ALU.mult, ALU.add).then_inc(s_cell, 1)

            def h_views(cut, u):
                slices = slice(*CUTS[cut])
                return h_now[u % 2][:, slices, :], h_parts[u % 2][:, slices, 0, :], h_parts[u % 2][:, slices, 1, :]

            def new_h(cut, u, turn):
                whole, high, low = h_views(cut, u)
                o3 = products[cut][:, 2 * GC[cut]:].rearrange("p (s b) -> p s b", b=N)
                tanh3 = tanh_c[cut][:, :].rearrange("p (s b) -> p s b", b=N)
                dve.wait_ge(s_tanh_c, turn)
                nc.vector.tensor_tensor(high, o3, tanh3, ALU.mult)
                nc.vector.tensor_tensor(whole, o3, tanh3, ALU.mult).then_inc(s_h_made, 1)

            def split_h(cut, u, turn):
                whole, high, low = h_views(cut, u)
                dve.wait_ge(s_h_made, turn)
                nc.vector.tensor_tensor(low, whole, high, ALU.subtract).then_inc(s_h[cut], 1)

            xt_reg = dve.alloc_register("xt_at")
            out_reg, x_reg = dve.alloc_register("out_at"), dve.alloc_register("x_at")
            for first, end, parts in SEGMENTS:
                with dve.Fori(first * GROUPS, end * GROUPS) as group_turn:
                    step0 = dve.snap(group_turn * UNROLL)
                    blk, group = group_turn // PIECES, group_turn % PIECES
                    for u in range(UNROLL):
                        step = step0 + u
                        turns = [step * C + cut + 1 for cut in range(C)]
                        sum_gates(0, step)
                        cell_products(0, turns[0])
                        new_cell(0, turns[0])
                        sum_gates(1, step)
                        new_h(0, u, turns[0])
                        cell_products(1, turns[1])
                        split_h(0, u, turns[0])
                        new_cell(1, turns[1])
                        sum_gates(2, step)
                        new_h(1, u, turns[1])
                        cell_products(2, turns[2])
                        split_h(1, u, turns[1])
                        new_cell(2, turns[2])
                        if u == 0 and parts & XT:
                            dve.reg_mov(xt_reg, group * (XT_RING * P) + (blk % XT_RING) * P)
                        if u == 1 and parts & OUT:
                            dve.reg_mov(out_reg, ((blk - 1) % 2) * D + group * P)
                            dve.reg_mov(x_reg, ((blk - 1) % XRING) * D + group * P)
                        new_h(2, u, turns[2])
                        split_h(2, u, turns[2])
                        if u == 0 and parts & XT:
                            keep_x_piece(group_turn + AHEAD * PIECES,
                                         dve.snap(xt_reg, min_val=0, max_val=(K * XT_RING - 1) * P))
                        if u == 1 and parts & OUT:
                            dve.wait_ge(s_out_psum, group_turn - (PIECES - 1))
                            dve.wait_ge(s_stored, 16 * N * blk)
                            add_x(dve.snap(out_reg, min_val=0, max_val=2 * D - P),
                                  dve.snap(x_reg, min_val=0, max_val=XRING * D - P), p_out[:, 0:P])
            dve.wait_ge(s_out_psum, (BLOCKS - 1) * PIECES + 1)
            dve.wait_ge(s_stored, 16 * N * BLOCKS)
            add_x((BLOCKS - 1) % 2 * D, (BLOCKS - 1) % XRING * D, p_out[:, :])


_INS = ["x", "cond_1024", "L0_cond_Wx", "L0_cond_Wh", "L0_cond_b"]
_OUTS = [((8, 512, 512), "float32")]


def kernel(**inputs):
    import numpy as _np
    import concourse.bacc as _bacc
    from concourse import mybir as _mybir
    from concourse.bass_utils import run_bass_kernel_spmd as _run

    nc = _bacc.Bacc("TRN2", target_bir_lowering=False, num_devices=1)
    arrays, args = {}, []
    for name in _INS:
        a = _np.ascontiguousarray(inputs[name])
        arrays[f"in_{name}_dram"] = a
        args.append(nc.dram_tensor(f"in_{name}_dram", a.shape, _mybir.dt.from_np(a.dtype), kind="ExternalInput").ap())
    for i, (shape, dtype) in enumerate(_OUTS):
        dt = _mybir.dt.from_np(_np.dtype(dtype))
        args.append(nc.dram_tensor(f"out_{i}_dram", shape, dt, kind="ExternalOutput").ap())
    lstm_residual_kernel(nc, *args)
    r = _run(nc, [arrays], core_ids=[0])
    got = tuple(r.results[0][f"out_{i}_dram"] for i in range(len(_OUTS)))
    return got[0]
```
